# Optimizing a Trainium2 kernel written in Bass

```python
import numpy as np
import jax
import jax.numpy as jnp

def _softmax(x, axis=-1):
    return jax.nn.softmax(x, axis=axis)

def _gelu(x):
    return jax.nn.gelu(x, approximate=True)

def _silu(x):
    return jax.nn.silu(x)

def _sigmoid(x):
    return jax.nn.sigmoid(x)

def _layernorm(x, axis=-1, eps=1e-05):
    m = jnp.mean(x, axis=axis, keepdims=True)
    v = jnp.var(x, axis=axis, keepdims=True)
    return (x - m) / jnp.sqrt(v + eps)

def _scatter_add(tgt, idx, src, axis=0):
    return tgt.at[idx].add(src)

def _segment_sum(src, seg, n):
    return jax.ops.segment_sum(src, seg, n)
kernel_name = 'mk_gnn_preln_d1_gnn_r64_8986c4'

def setup_inputs(seed: int=0):
    np.random.seed(seed)
    _w = jnp.asarray

    def _rec_inputs():
        import jax
        import jax.numpy as jnp
        _gk = jax.random.key(seed)
        x = -8.776e-05 + 1 * jax.random.normal(jax.random.fold_in(_gk, 1), (50000, 128), jnp.float32)
        src = jax.random.randint(jax.random.fold_in(_gk, 2), (25000,), 0, 50000, jnp.int32)
        dst = jax.random.randint(jax.random.fold_in(_gk, 3), (25000,), 0, 50000, jnp.int32)
        _o = jnp.argsort(dst, stable=True)
        src = src[_o]
        dst = dst[_o]
        edge_type_4 = jax.random.randint(jax.random.fold_in(_gk, 12), (25000,), 0, 4, jnp.int32)
        node_type_3 = jax.random.randint(jax.random.fold_in(_gk, 13), (50000,), 0, 3, jnp.int32)
        return (x, src, dst, edge_type_4, node_type_3)
    x, src, dst, edge_type_4, node_type_3 = _rec_inputs()

    def _L0_gnn_setup():
        import jax, jax.numpy as jnp
        import numpy as np
        import math
        N, E, D, T, R, H = (625, 10000, 128, 3, 4, 8)
        DK = D // H

        def _hgt_forward(node_inp, node_type, edge_index, edge_type, Wk, bk, Wq, bq, Wv, bv, Wa, ba, rel_pri, rel_att, rel_msg, skip, ln_g, ln_b):
            n = node_inp.shape[0]
            out_dim = Wk.shape[2]
            n_heads, d_k = (rel_att.shape[1], rel_att.shape[2])
            sqrt_dk = math.sqrt(d_k)
            rng = jnp.arange(n)

            def type_proj(W, b):
                all_t = jnp.einsum('ni,tio->tno', node_inp, W) + b[:, None, :]
                return all_t[node_type, rng]
            k = type_proj(Wk, bk)
            q = type_proj(Wq, bq)
            v = type_proj(Wv, bv)
            src, dst = (edge_index[0], edge_index[1])
            q_e = q[dst].reshape(-1, n_heads, d_k)
            k_e = k[src].reshape(-1, n_heads, d_k)
            v_e = v[src].reshape(-1, n_heads, d_k)
            k_rot = jnp.zeros_like(k_e)
            msg = jnp.zeros_like(v_e)
            n_rel = rel_att.shape[0]
            for r in range(n_rel):
                m = (edge_type == r)[:, None, None]
                k_rot = k_rot + jnp.where(m, jnp.einsum('ehd,hdf->ehf', k_e, rel_att[r]), 0.0)
                msg = msg + jnp.where(m, jnp.einsum('ehd,hdf->ehf', v_e, rel_msg[r]), 0.0)
            att = (q_e * k_rot).sum(-1) * rel_pri[edge_type] / sqrt_dk
            seg_max = jax.ops.segment_max(att, dst, num_segments=n)
            seg_max = jnp.where(jnp.isfinite(seg_max), seg_max, 0.0)
            ex = jnp.exp(att - seg_max[dst])
            denom = jax.ops.segment_sum(ex, dst, num_segments=n)[dst] + 1e-16
            alpha = ex / denom
            out_e = (msg * alpha[:, :, None]).reshape(-1, out_dim)
            aggr = jax.ops.segment_sum(out_e, dst, num_segments=n)
            h = jax.nn.gelu(aggr, approximate=False)
            trans_all = jnp.einsum('no,top->tnp', h, Wa) + ba[:, None, :]
            trans = trans_all[node_type, rng]
            a = jax.nn.sigmoid(skip)[node_type][:, None]
            res = trans * a + node_inp * (1.0 - a)
            mu = res.mean(-1, keepdims=True)
            var = ((res - mu) ** 2).mean(-1, keepdims=True)
            normed = (res - mu) * jax.lax.rsqrt(var + 1e-05)
            return normed * ln_g[node_type] + ln_b[node_type]
        key = jax.random.key(seed)
        ks = jax.random.split(key, 16)
        glorot = lambda k, shape, fan: jax.random.normal(k, shape, jnp.float32) * math.sqrt(2.0 / fan)
        inp = {'node_inp': jax.random.normal(ks[0], (N, D), jnp.float32), 'node_type': jax.random.randint(ks[1], (N,), 0, T), 'edge_index': jax.random.randint(ks[2], (2, E), 0, N), 'edge_type': jax.random.randint(ks[3], (E,), 0, R), 'Wk': glorot(ks[4], (T, D, D), 2 * D), 'bk': jnp.zeros((T, D), jnp.float32), 'Wq': glorot(ks[5], (T, D, D), 2 * D), 'bq': jnp.zeros((T, D), jnp.float32), 'Wv': glorot(ks[6], (T, D, D), 2 * D), 'bv': jnp.zeros((T, D), jnp.float32), 'Wa': glorot(ks[7], (T, D, D), 2 * D), 'ba': jnp.zeros((T, D), jnp.float32), 'rel_pri': jnp.ones((R, H), jnp.float32), 'rel_att': glorot(ks[8], (R, H, DK, DK), 2 * DK), 'rel_msg': glorot(ks[9], (R, H, DK, DK), 2 * DK), 'skip': jnp.ones((T,), jnp.float32), 'ln_g': jnp.ones((T, D), jnp.float32), 'ln_b': jnp.zeros((T, D), jnp.float32)}
        return inp
    _L0_gnn_all = _L0_gnn_setup()
    _L0_gnn_in = {k: v for k, v in _L0_gnn_all.items() if k in ('Wk', 'bk', 'Wq', 'bq', 'Wv', 'bv', 'Wa', 'ba', 'rel_pri', 'rel_att', 'rel_msg', 'skip', 'ln_g', 'ln_b')}
    del _L0_gnn_all
    return {'x': x, 'src': src, 'dst': dst, 'edge_type_4': edge_type_4, 'node_type_3': node_type_3, 'L0_gnn_Wk': _L0_gnn_in['Wk'], 'L0_gnn_bk': _L0_gnn_in['bk'], 'L0_gnn_Wq': _L0_gnn_in['Wq'], 'L0_gnn_bq': _L0_gnn_in['bq'], 'L0_gnn_Wv': _L0_gnn_in['Wv'], 'L0_gnn_bv': _L0_gnn_in['bv'], 'L0_gnn_Wa': _L0_gnn_in['Wa'], 'L0_gnn_ba': _L0_gnn_in['ba'], 'L0_gnn_rel_pri': _L0_gnn_in['rel_pri'], 'L0_gnn_rel_att': _L0_gnn_in['rel_att'], 'L0_gnn_rel_msg': _L0_gnn_in['rel_msg'], 'L0_gnn_skip': _L0_gnn_in['skip'], 'L0_gnn_ln_g': _L0_gnn_in['ln_g'], 'L0_gnn_ln_b': _L0_gnn_in['ln_b']}

def reference(x, src, dst, edge_type_4, node_type_3, L0_gnn_Wk, L0_gnn_bk, L0_gnn_Wq, L0_gnn_bq, L0_gnn_Wv, L0_gnn_bv, L0_gnn_Wa, L0_gnn_ba, L0_gnn_rel_pri, L0_gnn_rel_att, L0_gnn_rel_msg, L0_gnn_skip, L0_gnn_ln_g, L0_gnn_ln_b):
    import jax
    import jax.numpy as jnp

    def _L0_gnn_ref(node_inp, node_type, edge_index, edge_type, Wk, bk, Wq, bq, Wv, bv, Wa, ba, rel_pri, rel_att, rel_msg, skip, ln_g, ln_b):
        import jax, jax.numpy as jnp
        import numpy as np
        import math
        N, E, D, T, R, H = (625, 10000, 128, 3, 4, 8)
        DK = D // H

        def _hgt_forward(node_inp, node_type, edge_index, edge_type, Wk, bk, Wq, bq, Wv, bv, Wa, ba, rel_pri, rel_att, rel_msg, skip, ln_g, ln_b):
            n = node_inp.shape[0]
            out_dim = Wk.shape[2]
            n_heads, d_k = (rel_att.shape[1], rel_att.shape[2])
            sqrt_dk = math.sqrt(d_k)
            rng = jnp.arange(n)

            def type_proj(W, b):
                all_t = jnp.einsum('ni,tio->tno', node_inp, W) + b[:, None, :]
                return all_t[node_type, rng]
            k = type_proj(Wk, bk)
            q = type_proj(Wq, bq)
            v = type_proj(Wv, bv)
            src, dst = (edge_index[0], edge_index[1])
            q_e = q[dst].reshape(-1, n_heads, d_k)
            k_e = k[src].reshape(-1, n_heads, d_k)
            v_e = v[src].reshape(-1, n_heads, d_k)
            k_rot = jnp.zeros_like(k_e)
            msg = jnp.zeros_like(v_e)
            n_rel = rel_att.shape[0]
            for r in range(n_rel):
                m = (edge_type == r)[:, None, None]
                k_rot = k_rot + jnp.where(m, jnp.einsum('ehd,hdf->ehf', k_e, rel_att[r]), 0.0)
                msg = msg + jnp.where(m, jnp.einsum('ehd,hdf->ehf', v_e, rel_msg[r]), 0.0)
            att = (q_e * k_rot).sum(-1) * rel_pri[edge_type] / sqrt_dk
            seg_max = jax.ops.segment_max(att, dst, num_segments=n)
            seg_max = jnp.where(jnp.isfinite(seg_max), seg_max, 0.0)
            ex = jnp.exp(att - seg_max[dst])
            denom = jax.ops.segment_sum(ex, dst, num_segments=n)[dst] + 1e-16
            alpha = ex / denom
            out_e = (msg * alpha[:, :, None]).reshape(-1, out_dim)
            aggr = jax.ops.segment_sum(out_e, dst, num_segments=n)
            h = jax.nn.gelu(aggr, approximate=False)
            trans_all = jnp.einsum('no,top->tnp', h, Wa) + ba[:, None, :]
            trans = trans_all[node_type, rng]
            a = jax.nn.sigmoid(skip)[node_type][:, None]
            res = trans * a + node_inp * (1.0 - a)
            mu = res.mean(-1, keepdims=True)
            var = ((res - mu) ** 2).mean(-1, keepdims=True)
            normed = (res - mu) * jax.lax.rsqrt(var + 1e-05)
            return normed * ln_g[node_type] + ln_b[node_type]
        return _hgt_forward(node_inp, node_type, edge_index, edge_type, Wk, bk, Wq, bq, Wv, bv, Wa, ba, rel_pri, rel_att, rel_msg, skip, ln_g, ln_b)
    edge_index = jnp.stack([src, dst])
    h = jnp.maximum(_layernorm(x, axis=-1), 0.0)
    x = x + _L0_gnn_ref(h, node_type_3, edge_index, edge_type_4, L0_gnn_Wk, L0_gnn_bk, L0_gnn_Wq, L0_gnn_bq, L0_gnn_Wv, L0_gnn_bv, L0_gnn_Wa, L0_gnn_ba, L0_gnn_rel_pri, L0_gnn_rel_att, L0_gnn_rel_msg, L0_gnn_skip, L0_gnn_ln_g, L0_gnn_ln_b)
    return x

_drawn_inputs = setup_inputs


def setup_inputs(seed=0):
    import zlib

    import numpy as np

    out = dict(_drawn_inputs(seed))
    spreads = {'L0_gnn_bk': (0.0, 0.8),
     'L0_gnn_bq': (0.0, 0.8),
     'L0_gnn_bv': (0.0, 0.1),
     'L0_gnn_ba': (0.0, 0.1),
     'L0_gnn_rel_pri': (1.0, 0.6),
     'L0_gnn_skip': (1.0, 0.2),
     'L0_gnn_ln_g': (1.0, 0.2),
     'L0_gnn_ln_b': (0.0, 0.1)}
    factors = {}
    for name, (base, spread) in spreads.items():
        noise = np.random.default_rng([zlib.crc32(name.encode()), seed]).standard_normal(out[name].shape)
        drawn = base * np.exp(spread * noise) if base else spread * noise
        out[name] = jnp.asarray(drawn.astype(out[name].dtype))
    for name, factor in factors.items():
        out[name] = (out[name] * factor).astype(out[name].dtype)
    return out
```

```python
import math

import concourse.bass as bass
from concourse import mybir
from contextlib import ExitStack

F32 = mybir.dt.float32
BF16 = mybir.dt.bfloat16
I32 = mybir.dt.int32
ALU = mybir.AluOpType
ACT = mybir.ActivationFunctionType

P = 128
G = 4
W = P * G
LN_EPS = 1e-05
DEN_EPS = 1e-16
FAR = 1e30
SKIP_ROW = 1 << 16
TAB = 96


class Step:

    def __init__(self, first, ring, trip=0):
        self.first, self.ring, self.trip = first, ring, trip
        self.c = first + ring * trip
        self.slot = first % ring
        self.round = first // ring + trip

    def back(self, k):
        return Step(self.first - k, self.ring, self.trip)


def gnn_layer(nc, x, src, dst, etype, ntype, Wk, bk, Wq, bq, Wv, bv, Wa, ba,
              rel_pri, rel_att, rel_msg, skip, ln_g, ln_b, out):
    N, D = x.shape
    E = src.shape[0]
    T = Wk.shape[0]
    R, H, DK, _ = rel_att.shape
    assert D == P and H * DK == D and N % 16 == 0
    NB = -(-N // W)
    NC = -(-E // W)
    NT = NC * G
    E_LAST = E - (NC - 1) * W
    LO = min(NT, P)
    HI = NT - LO
    FULL = E // P
    REST = E - FULL * P
    x_ring, e_ring = 4, 3

    ctx = ExitStack()
    with ctx:
        def sb(name, shape, dt=F32):
            return ctx.enter_context(nc.sbuf_tensor(name, shape, dt))

        sems = {}

        def sem(name):
            if name not in sems:
                sems[name] = ctx.enter_context(nc.semaphore(name))
            return sems[name]

        wk, wq, wv, wa = (sb(n, [P, T, D]) for n in ("wk", "wq", "wv", "wa"))
        att_w = sb("att_w", [P, R, D])
        msg_w = sb("msg_w", [P, R, D])
        pri = sb("pri", [P, R])
        ident = sb("ident", [P, P])
        ident16 = sb("ident16", [P, P], BF16)
        head_ones = sb("head_ones", [P, P])
        NTAB = 6
        tab = sb("tab", [TAB, NTAB, D])
        tab_hi = sb("tab_hi", [TAB, NTAB, D], BF16)
        tab_mid = sb("tab_mid", [TAB, NTAB, D], BF16)
        tab_lo = sb("tab_lo", [TAB, NTAB, D], BF16)
        tab_r1 = sb("tab_r1", [TAB, NTAB, D])
        tab_r2 = sb("tab_r2", [TAB, NTAB, D])
        tab16 = sb("tab16", [TAB, NTAB, D], BF16)
        type_of_row = sb("type_of_row", [TAB, P])
        spread_type = sb("spread_type", [TAB, P], BF16)
        gate_row = sb("gate_row", [TAB, 3])
        gate = sb("gate", [P, 4, T])
        minus_half = sb("minus_half", [P, 2 * G])

        rows_i = sb("rows_i", [P, 2, 3, P], I32)
        rows_f = sb("rows_f", [P, 2, 3, P])
        cols_f = sb("cols_f", [P, 3, NT])
        last_of_run = sb("last_of_run", [P, NT])
        index = sb("index", [P, NC, 3, G], I32)

        nt_all = sb("nt_all", [P, NB * G], I32)
        keep_n = sb("keep_n", [P, NB * G])
        arena = sb("arena", [P, NB * G * TAB // 2])
        hot_n = arena[:].bitcast(BF16).rearrange("p (n t) -> p n t", t=TAB)

        def carve(k, n):
            return arena[:, k * W:(k + n) * W].rearrange("p (n w) -> p n w", w=W)

        hsm, hdm = carve(0, T), carve(T, T)
        km, vm = carve(2 * T, R), carve(2 * T + R, R)
        gm = carve(2 * T + 2 * R, T)
        xa = sb("xa", [P, x_ring, G, D])
        oa = sb("oa", [P, x_ring, G, D])
        bst = sb("bst", [P, 2 * G, 6])
        bst2 = sb("bst2", [P, G, 6])
        mv1 = sb("mv1", [P, x_ring, 2 * G, 2])
        mv2 = sb("mv2", [P, x_ring, G, 2])
        sc1 = sb("sc1", [P, x_ring, 6, 2 * G])
        sc2 = sb("sc2", [P, x_ring, 4, G])
        hc = sb("hc", [P, x_ring, G, D])
        hot_t = sb("hot_t", [TAB, x_ring, 2, W], BF16)
        nm = sb("nm", [P, G, D])
        yg = sb("yg", [P, G, D])

        psum = [ctx.enter_context(nc.psum_tensor(f"bank{i}", [P, W], F32)) for i in range(8)]

        block = ctx.enter_context(nc.Block())

        def after(eng, name, value):
            if not isinstance(value, int) or value > 0:
                eng.wait_ge(sem(name), value)

        def hold(eng, name):
            eng.sem_inc(sem(name), 1)

        def node_steps(eng, body):
            head, trips = 4, (NB - 7) // x_ring
            for j in range(head):
                body(Step(j, x_ring))
            with eng.Fori(0, trips) as i:
                for u in range(x_ring):
                    body(Step(head + u, x_ring, i))
            for j in range(head + trips * x_ring, NB + 2):
                body(Step(j, x_ring))

        def edge_steps(eng, body):
            head, trips = 3, (NC - 6) // e_ring
            for j in range(head):
                body(Step(j, e_ring))
            with eng.Fori(0, trips) as i:
                for u in range(e_ring):
                    body(Step(head + u, e_ring, i))
            for j in range(head + trips * e_ring, NC + 1):
                body(Step(j, e_ring))

        def live(s, k, n):
            return isinstance(s.c, int) and 0 <= s.c - k < n or not isinstance(s.c, int)

        def flat(t):
            return t.rearrange("p g d -> p (g d)")

        icur = sb("icur", [P, e_ring, 2, G], I32)
        scur = sb("scur", [P, e_ring, G], I32)
        xs = sb("xs", [P, e_ring, G, D])
        xd = sb("xd", [P, e_ring, G, D])
        tys = sb("tys", [P, e_ring, 2, G], I32)
        keep_e = sb("keep_e", [P, e_ring, G])
        hot_e = sb("hot_e", [P, 2, G, TAB], BF16)
        hs = sb("hs", [P, G, D])
        hd = sb("hd", [P, G, D])
        tyb = sb("tyb", [P, e_ring, 2, W], BF16)
        etb = sb("etb", [P, e_ring, W], I32)
        dstb = sb("dstb", [P, e_ring, W + 1], I32)
        same = sb("same", [P, W])
        cut = sb("cut", [P, e_ring, W])
        qs = carve(17, 1)[:, 0]
        prod = carve(18, 1)[:, 0]
        top = sb("top", [P, W + 1])
        tA = carve(19, 1)[:, 0]
        te = carve(28, 2)
        ce = carve(30, 2)
        pm = carve(20, 1)[:, 0]
        run = sb("run", [P, 2, W + 1])
        den = carve(21, 1)[:, 0]
        lnd = carve(22, 1)[:, 0]
        inv0 = carve(23, 1)[:, 0]
        nt1 = carve(24, 1)[:, 0]
        nt2 = carve(25, 1)[:, 0]
        ag = carve(26, 1)[:, 0]
        ge = carve(27, 1)[:, 0]
        nme = carve(32, 1)[:, 0].rearrange("p (g d) -> p g d", g=G)
        yge = carve(33, 1)[:, 0].rearrange("p (g d) -> p g d", g=G)
        oe = oa[:, 0:e_ring]

        TAB_A, TAB_G, TAB_B, TAB_K, TAB_V, TAB_Q = range(NTAB)
        small_loads = 0

        @block.sync
        def _(sp):
            w = sem("weights_in")
            nonlocal small_loads
            sp.wait_ge(sem("cleared"), 5)
            for k, (v, shift) in enumerate(((src, 0), (dst, 0), (dst, 1))):
                sp.dma_start(rows_i[0:LO, 0, k, :],
                             v[shift:shift + LO * P].rearrange("(t e) -> t e", e=P)).then_inc(sem("index_in"), 16)
                n = FULL - LO if REST or not shift else FULL - LO - 1
                sp.dma_start(rows_i[0:n, 1, k, :],
                             v[shift + LO * P:shift + (LO + n) * P].rearrange("(t e) -> t e", e=P))\
                    .then_inc(sem("index_in"), 16)
                tail = v[shift + (LO + n) * P:E]
                sp.dma_start(rows_i[n:n + 1, 1, k, 0:tail.shape[0]],
                             tail.rearrange("(t e) -> t e", t=1)).then_inc(sem("index_in"), 16)
            for b in range(NB):
                base = min(b * W, N - W)
                sp.dma_start(nt_all[:, b * G:(b + 1) * G],
                             ntype[base:base + W].rearrange("(p j) -> p j", j=G)).then_inc(sem("types_in"), 16) \
                    if b == NB - 1 else None
            sp.dma_start(nt_all[:, 0:(NB - 1) * G].rearrange("p (b j) -> p b j", j=G),
                         ntype[0:(NB - 1) * W].rearrange("(b p j) -> p b j", p=P, j=G)).then_inc(sem("types_in"), 16)
            for t, (dst_w, src_w) in enumerate(((wk, Wk), (wq, Wq), (wv, Wv), (wa, Wa))):
                sp.dma_start(dst_w[:, :, :], src_w.rearrange("t i o -> i t o")).then_inc(w, 16)
            sp.dma_start(gate[:, 0, :], skip.rearrange("(a t) -> a t", a=1).to_broadcast([P, T])).then_inc(w, 16)
            for part in range(3):
                for k, v in enumerate((ba, ln_g, ln_b, bk, bv, bq)):
                    sp.dma_start(tab[32 * part:32 * part + T, k, :], v).then_inc(w, 16)
                sp.dma_start(gate_row[32 * part:32 * part + T, 0:1],
                             skip.rearrange("(t a) -> t a", a=1)).then_inc(w, 16)
            for h in range(H):
                rows = slice(h * DK, (h + 1) * DK)
                sp.dma_start(att_w[rows, :, rows], rel_att[:, h].rearrange("r d f -> d r f")).then_inc(w, 16)
                sp.dma_start(msg_w[rows, :, rows], rel_msg[:, h].rearrange("r d f -> d r f")).then_inc(w, 16)
                sp.dma_start(pri[rows, :],
                             rel_pri[:, h:h + 1].rearrange("r a -> a r").to_broadcast([DK, R]),
                             allow_slow_non_contiguous=True).then_inc(w, 16)

            def load_x(base, s):
                sp.dma_start(xa[:, s.slot], x[bass.ds(base, W), :].rearrange("(p j) d -> p j d", j=G))\
                    .then_inc(sem(f"x_in{s.slot}"), 16)

            def store_o(base, s):
                sp.dma_start(out[bass.ds(base, W), :].rearrange("(p j) d -> p j d", j=G), oa[:, s.slot])\
                    .then_inc(sem(f"o_out{s.slot}"), 16)

            ahead = 2

            def body(s):
                if isinstance(s.c, int):
                    nxt = [s.c] if s.c + ahead < NB and s.c >= 0 else []
                    first = range(ahead) if s.c == 0 else []
                    for b in first:
                        load_x(b * W, Step(b, x_ring))
                    if nxt:
                        f = Step(s.first + ahead, x_ring, s.trip)
                        after(sp, "n_xb", s.c + ahead - x_ring + 1)
                        load_x(min(f.c * W, N - W), f)
                else:
                    f = Step(s.first + ahead, x_ring, s.trip)
                    after(sp, "n_xb", s.c + ahead - x_ring + 1)
                    load_x(f.c * W, f)
                if live(s, 2, NB):
                    p = s.back(2)
                    after(sp, "n_out", p.c + 1)
                    if isinstance(p.c, int) and p.c == NB - 1:
                        q = p.back(1)
                        sp.wait_ge(sem(f"o_out{q.slot}"), 16 * (q.round + 1))
                        store_o(N - W, p)
                    else:
                        store_o(p.c * W, p)

            node_steps(sp, body)
            for slot in range(x_ring):
                n = len(range(slot, NB, x_ring))
                sp.wait_ge(sem(f"o_out{slot}"), 16 * n)
            sp.sem_inc(sem("nodes_stored"), 1)

        def load_edge_rows(eng, s):
            n = W if not isinstance(s.c, int) or s.c < NC - 1 else E_LAST
            eng.dma_start(etb[:, s.slot, 0:n],
                          etype[bass.ds(s.c * W, n)].rearrange("(a e) -> a e", a=1).to_broadcast([P, n]))\
                .then_inc(sem(f"e_in{s.slot}"), 16)
            lead = 0 if isinstance(s.c, int) and s.c == 0 else 1
            eng.dma_start(dstb[:, s.slot, 1 - lead:n + 1],
                          dst[bass.ds(s.c * W - lead, n + lead)].rearrange("(a e) -> a e", a=1).to_broadcast([P, n + lead]))\
                .then_inc(sem(f"e_in{s.slot}"), 16)

        @block.gpsimd
        def _(pool):
            for t in (rows_i, tab, att_w, msg_w):
                pool.memset(t[:], 0 if t is not rows_i else -1).then_inc(sem("cleared"), 1)
            pool.memset(minus_half[:], -0.5).then_inc(sem("const"), 1)
            pool.memset(gate_row[:], 0.0).then_inc(sem("cleared"), 1)
            pool.memset(arena[:], 0.0).then_inc(sem("hot_cleared"), 1)
            pool.memset(hot_e[:], 0.0).then_inc(sem("hot_cleared"), 1)
            for t in (ident, ident16):
                pool.memset(t[:], 0.0).then_inc(sem("pool_prep"), 1)
            pool.memset(head_ones[:], 1.0).then_inc(sem("pool_prep"), 1)
            pool.wait_ge(sem("pool_prep"), 3)
            for t in (ident, ident16):
                pool.affine_select(out=t[:], in_=t[:], compare_op=ALU.not_equal, fill=1.0, base=0,
                                   pattern=[[-1, P]], channel_multiplier=1).then_inc(sem("const"), 1)
            ho = head_ones[:].rearrange("p (h d) -> p h d", d=DK)
            pool.affine_select(out=ho, in_=ho, compare_op=ALU.is_ge, fill=0.0, base=0,
                               pattern=[[-DK, H], [0, DK]], channel_multiplier=1).then_inc(sem("pool_prep"), 1)
            pool.wait_ge(sem("pool_prep"), 4)
            pool.affine_select(out=ho, in_=ho, compare_op=ALU.is_ge, fill=0.0, base=DK - 1,
                               pattern=[[DK, H], [0, DK]], channel_multiplier=-1).then_inc(sem("const"), 1)
            pool.iota(type_of_row[:], pattern=[[0, P]], base=0, channel_multiplier=1,
                      allow_small_or_imprecise_dtypes=True).then_inc(sem("const"), 1)

            def small(op, sem_name, *args, **kw):
                op(*args, **kw).then_inc(sem(sem_name), 1)

            def norm_scalars(name, step_count, per, mv, sc, n, keep, keep_at, done):
                k = [0]

                def link(ins):
                    k[0] += 1
                    ins.then_inc(sem(name), 1)
                    after(pool, name, step_count * per + k[0])
                    hold(pool, "pool_turns")

                hold(pool, "pool_turns")
                link(pool.tensor_scalar(sc[:, 0, 0:n], mv[:, :, 1], LN_EPS, None, ALU.add))
                link(pool.tensor_tensor(sc[:, 1, 0:n], sc[:, 0, 0:n], minus_half[:, 0:n], ALU.pow))
                if keep is not None:
                    a = keep_at
                    m = keep.shape[1]
                    link(pool.tensor_tensor(sc[:, 4, a:a + m], sc[:, 1, a:a + m], keep, ALU.mult))
                link(pool.tensor_tensor(sc[:, 2, 0:n], mv[:, :, 0], sc[:, 1, 0:n], ALU.mult))
                if keep is not None:
                    link(pool.tensor_scalar(sc[:, 3, 0:n], sc[:, 2, 0:n], -1.0, None, ALU.mult))
                    pool.tensor_tensor(sc[:, 5, a:a + m], sc[:, 3, a:a + m], keep, ALU.mult)\
                        .then_inc(sem(done), 1)
                else:
                    pool.tensor_scalar(sc[:, 3, 0:n], sc[:, 2, 0:n], -1.0, None, ALU.mult)\
                        .then_inc(sem(done), 1)

            pool.wait_ge(sem("keep_ready"), 1)

            def node_body(s):
                if live(s, 0, NB):
                    after(pool, "n_mv1", s.c + 1)
                    norm_scalars("pn1", s.c, 5, mv1[:, s.slot, 0:G, :], sc1[:, s.slot], G,
                                 keep_n[:, bass.ds(s.c * G, G)], 0, "n_sc1")
                if live(s, 1, NB):
                    p = s.back(1)
                    after(pool, "n_mv2", p.c + 1)
                    norm_scalars("pn2", p.c, 3, mv2[:, p.slot], sc2[:, p.slot], G, None, 0, "n_sc2")
            node_steps(pool, node_body)

            pool.wait_ge(sem("index_ready"), 3)

            def gathers(s):
                pool.tensor_copy(icur[:, s.slot], index[:, s.c, 0:2, :] if isinstance(s.c, int) else
                                 index[:, bass.ds(s.c, 1), 0:2, :].rearrange("p a k g -> p (a k) g"))\
                    .then_inc(sem("icur_ready"), 1)
                after(pool, "icur_ready", s.c + 1)
                hold(pool, "pool_turns")
                for k, (rows, name) in enumerate(((xs, "g_src"), (xd, "g_dst"))):
                    for g in range(G):
                        off = bass.IndirectOffsetOnAxis(ap=icur[:, s.slot, k, g:g + 1], axis=0)
                        pool.indirect_dma_start(out=rows[:, s.slot, g, :], out_offset=None, in_=x,
                                                in_offset=off).then_inc(sem(f"{name}{s.slot}"), 16)
                        pool.indirect_dma_start(out=tys[:, s.slot, k, g:g + 1], out_offset=None,
                                                in_=ntype.rearrange("(n a) -> n a", a=1),
                                                in_offset=off).then_inc(sem(f"{name}{s.slot}"), 16)

            def scatter(s):
                pool.tensor_copy(scur[:, s.slot], index[:, s.c, 2, :] if isinstance(s.c, int) else
                                 index[:, bass.ds(s.c, 1), 2, :].rearrange("p a g -> p (a g)"))\
                    .then_inc(sem("scur_ready"), 1)
                after(pool, "scur_ready", s.c + 1)
                hold(pool, "pool_turns")
                after(pool, "e_out", s.c + 1)
                hold(pool, "pool_turns")
                for g in range(G):
                    pool.indirect_dma_start(
                        out=out, out_offset=bass.IndirectOffsetOnAxis(ap=scur[:, s.slot, g:g + 1], axis=0),
                        in_=oe[:, s.slot, g, :], in_offset=None, bounds_check=N - 1, oob_is_err=False)\
                        .then_inc(sem(f"scattered{s.slot}"), 16)

            gathers(Step(0, e_ring))
            pool.wait_ge(sem("nodes_stored"), 1)

            def edge_body(s):
                if live(s, 0, NC):
                    after(pool, "e_mv1", s.c + 1)
                    norm_scalars("pe1", s.c, 5, mv1[:, s.slot], sc1[:, s.slot], 2 * G,
                                 keep_e[:, s.slot], G, "e_sc1")
                if live(s, 2, NC):
                    p = s.back(2)
                    after(pool, f"scattered{p.slot}", 16 * G * p.round)
                    scatter(p)
                if live(s, -1, NC):
                    n = s.back(-1)
                    after(pool, "e_xb", n.c - e_ring + 1)
                    after(pool, f"g_src{n.slot}", 16 * 2 * G * n.round)
                    after(pool, f"g_dst{n.slot}", 16 * 2 * G * n.round)
                    gathers(n)
                if live(s, 1, NC):
                    p = s.back(1)
                    after(pool, "e_mv2", p.c + 1)
                    norm_scalars("pe2", p.c, 3, mv2[:, p.slot], sc2[:, p.slot], G, None, 0, "e_sc2")
            edge_steps(pool, edge_body)
            last = Step(NC - 1, e_ring)
            after(pool, f"scattered{last.slot}", 16 * G * last.round)
            scatter(last)
            for slot in range(e_ring):
                n = len(range(slot, NC, e_ring))
                pool.wait_ge(sem(f"scattered{slot}"), 16 * G * n)

        @block.scalar
        def _(act):
            act.wait_ge(sem("weights_in"), W_LOADS)
            act.activation(gate[:, 1, :], gate[:, 0, :], ACT.Exp, scale=-1.0).then_inc(sem("gate_exp"), 1)
            act.activation(gate_row[:, 1:2], gate_row[:, 0:1], ACT.Exp, scale=-1.0).then_inc(sem("gate_exp"), 1)
            for slot in range(e_ring):
                if slot == 0:
                    act.wait_ge(sem("dve_init"), 1)
                load_edge_rows(act, Step(slot, e_ring))

            def node_body(s):
                if live(s, 0, NB):
                    after(act, f"x_in{s.slot}", 16 * (s.round + 1))
                    after(act, "n_sc1", s.c + 1)
                    after(act, "n_res", s.c - x_ring + 1)
                    for g in range(G):
                        ins = act.activation(hc[:, s.slot, g], xa[:, s.slot, g], ACT.Relu,
                                             bias=sc1[:, s.slot, 5, g:g + 1], scale=sc1[:, s.slot, 4, g:g + 1])
                    ins.then_inc(sem("n_hc"), 1)
                    after(act, "n_hot_ps", s.c + 1)
                    act.activation(hot_t[:, s.slot, 0], psum[6 + s.slot % 2][0:TAB, 0:W // 2].bitcast(BF16),
                                   ACT.Copy).then_inc(sem("n_hot"), 1)
                if live(s, 1, NB):
                    p = s.back(1)
                    after(act, "n_sc2", p.c + 1)
                    after(act, "n_res", p.c + 1)
                    after(act, "n_y", p.c)
                    for g in range(G):
                        ins = act.activation(nm[:, g], psum[p.slot % 2][:, g * P:(g + 1) * P], ACT.Identity,
                                             bias=sc2[:, p.slot, 3, g:g + 1], scale=sc2[:, p.slot, 1, g:g + 1])
                    ins.then_inc(sem("n_nm"), 1)
            node_steps(act, node_body)

            def edge_body(s):
                c, p = s, s.back(1)
                if live(s, 1, NC):
                    after(act, "e_te", p.c + 1)
                    after(act, "e_run", p.c)
                    act.activation(flat(ce), flat(te), ACT.Exp).then_inc(sem("e_ce"), 1)
                if live(s, 0, NC):
                    after(act, f"g_src{c.slot}", 16 * 2 * G * (c.round + 1))
                    after(act, f"g_dst{c.slot}", 16 * 2 * G * (c.round + 1))
                    after(act, "e_sc1", c.c + 1)
                    after(act, "e_turned", c.c)
                    for g in range(G):
                        act.activation(hs[:, g], xs[:, c.slot, g], ACT.Relu,
                                       bias=sc1[:, c.slot, 3, g:g + 1], scale=sc1[:, c.slot, 1, g:g + 1])
                        act.activation(hd[:, g], xd[:, c.slot, g], ACT.Relu,
                                       bias=sc1[:, c.slot, 3, G + g:G + g + 1],
                                       scale=sc1[:, c.slot, 1, G + g:G + g + 1])
                        ins = act.activation(hc[:, c.slot, g], xd[:, c.slot, g], ACT.Relu,
                                             bias=sc1[:, c.slot, 5, G + g:G + g + 1],
                                             scale=sc1[:, c.slot, 4, G + g:G + g + 1])
                    ins.then_inc(sem("e_h"), 1)
                    after(act, "e_turned", c.c + 1)
                    act.activation(hot_t[:, c.slot], psum[2][0:TAB, :].bitcast(BF16).rearrange("p (k e) -> p k e", k=2),
                                   ACT.Copy).then_inc(sem("e_hot"), 1)
                if live(s, 1, NC):
                    after(act, "e_den", p.c + 1)
                    act.activation(lnd, den, ACT.Ln).then_inc(sem("e_lnd"), 1)
                    after(act, "e_lnd", p.c + 1)
                    act.activation(inv0, lnd, ACT.Exp, scale=-1.0).then_inc(sem("e_inv0"), 1)
                if live(s, 0, NC):
                    after(act, "e_spread", c.c + 1)
                    act.activation(tyb[:, c.slot, 0], psum[2][:], ACT.Copy).then_inc(sem("e_tyb"), 1)
                    act.activation(tyb[:, c.slot, 1], psum[3][:], ACT.Copy).then_inc(sem("e_tyb"), 1)
                    after(act, "e_same", c.c + 1)
                    act.activation(cut[:, c.slot], same[:], ACT.Copy, bias=-FAR, scale=FAR).then_inc(sem("e_cut"), 1)
                if live(s, 1, NC):
                    after(act, "e_ag", p.c + 1)
                    act.activation(ge, ag, ACT.Gelu).then_inc(sem("e_ge"), 1)
                if live(s, 0, NC):
                    after(act, "e_q", c.c + 1)
                    act.activation(qs, psum[1][:], ACT.Copy).then_inc(sem("e_qs"), 1)
                if live(s, 1, NC):
                    after(act, "e_sc2", p.c + 1)
                    for g in range(G):
                        ins = act.activation(nme[:, g], psum[6][:, g * P:(g + 1) * P], ACT.Identity,
                                             bias=sc2[:, p.slot, 3, g:g + 1], scale=sc2[:, p.slot, 1, g:g + 1])
                    ins.then_inc(sem("e_nm"), 1)
                if live(s, -2, NC) and (not isinstance(s.c, int) or s.c >= 1):
                    n = s.back(-2)
                    after(act, "e_vm", n.c - e_ring + 1)
                    after(act, "e_same", n.c - e_ring + 1)
                    load_edge_rows(act, n)
            edge_steps(act, edge_body)

        @block.tensor
        def _(pe):
            pe.wait_ge(sem("const"), 5)
            pe.wait_ge(sem("rows_ready"), 1)
            for k in range(3):
                pe.transpose(psum[k][:, 0:LO], rows_f[0:LO, 0, k, :], ident[0:LO, 0:LO])
                pe.transpose(psum[k][:, LO:NT], rows_f[0:HI, 1, k, :], ident[0:HI, 0:HI])\
                    .then_inc(sem("cols_ps"), 1)
            pe.wait_ge(sem("tables_ready"), 1)
            pe.wait_ge(sem("index_ready"), 3)
            pe.wait_ge(sem("hot_n_ready"), 1)

            def by_type(ps, hot, table, start, stop):
                for g in range(G):
                    ins = pe.matmul(ps[:, g * P:(g + 1) * P], hot[:, g * P:(g + 1) * P], tab16[:, table, :],
                                    start=start, stop=stop, skip_group_check=True)
                return ins

            def node_body(s):
                if live(s, 0, NB):
                    after(pe, "n_hot", s.c - 1)
                    ps = psum[6 + s.slot % 2][0:TAB, 0:W // 2].bitcast(BF16)
                    for g in range(G):
                        ins = pe.transpose(ps[:, g * P:(g + 1) * P],
                                           hot_n[:, bass.ds(s.c * G + g, 1), :].rearrange("p a t -> p (a t)"),
                                           ident16[:])
                    ins.then_inc(sem("n_hot_ps"), 1)
                if live(s, 1, NB):
                    p = s.back(1)
                    hot = hot_t[:, p.slot, 0]
                    par = p.slot % 2
                    after(pe, "n_hc", p.c + 1)
                    after(pe, "n_hot", p.c + 1)
                    after(pe, "n_nm", p.c - 1)
                    pe.matmul(psum[par][:], ident[:], flat(hc[:, p.slot]), start=True, stop=False, skip_group_check=True)
                    by_type(psum[par], hot, TAB_A, False, True).then_inc(sem("n_res"), 1)
                    after(pe, "n_y", p.c - 1)
                    by_type(psum[2 + par], hot, TAB_G, True, True).then_inc(sem("n_g"), 1)
                    after(pe, "n_out", p.c - 1)
                    pe.matmul(psum[4 + par][:], ident[:], flat(xa[:, p.slot]), start=True, stop=False, skip_group_check=True)
                    by_type(psum[4 + par], hot, TAB_B, False, True).then_inc(sem("n_xb"), 1)
            node_steps(pe, node_body)
            pe.wait_ge(sem("n_out"), NB)

            def edge_body(s):
                c, p = s, s.back(1)
                if live(s, 0, NC):
                    after(pe, "e_h", c.c + 1)
                    after(pe, "e_km", c.c)
                    after(pe, "e_vm", c.c)
                    after(pe, "e_qs", c.c)
                    for g in range(G):
                        pe.transpose(psum[0][:, g * P:(g + 1) * P], hs[:, g], ident[:])
                        pe.transpose(psum[1][:, g * P:(g + 1) * P], hd[:, g], ident[:])
                    after(pe, "e_hot16", 2 * (c.c + 1))
                    for k in range(2):
                        for g in range(G):
                            ins = pe.transpose(psum[2][0:TAB, :].bitcast(BF16)[:, k * W + g * P:k * W + (g + 1) * P],
                                               hot_e[:, k, g, :], ident16[:])
                    ins.then_inc(sem("e_turned"), 1)
                    after(pe, "e_hot", c.c + 1)
                    after(pe, "e_prod", c.c)
                    pe.matmul(psum[2][:], spread_type[:], hot_t[:, c.slot, 0], start=True, stop=True)
                    pe.matmul(psum[3][:], spread_type[:], hot_t[:, c.slot, 1], start=True, stop=True)\
                        .then_inc(sem("e_spread"), 1)

                    def project(ps, weights, table, rows, k):
                        for t in range(T):
                            pe.matmul(ps[:], weights[:, t], rows[:, t], start=(t == 0), stop=False)
                        return pe.matmul(ps[:], tab16[:, table, :], hot_t[:, c.slot, k], start=False, stop=True)

                    after(pe, "e_hsm", c.c + 1)
                    project(psum[0], wk, TAB_K, hsm, 0).then_inc(sem("e_k"), 1)
                    after(pe, "e_tyb", 2 * (c.c + 1))
                    project(psum[2], wv, TAB_V, hsm, 0).then_inc(sem("e_v"), 1)
                if live(s, 1, NC):
                    after(pe, "e_gm", p.c + 1)
                    after(pe, "e_out", p.c)
                    pe.matmul(psum[6][:], ident[:], flat(hc[:, p.slot]), start=True, stop=False, skip_group_check=True)
                    for t in range(T):
                        for g in range(G):
                            pe.matmul(psum[6][:, g * P:(g + 1) * P], gm[:, t, g * P:(g + 1) * P], wa[:, t],
                                      start=False, stop=False, skip_group_check=True)
                    by_type(psum[6], hot_t[:, p.slot, 1], TAB_A, False, True).then_inc(sem("e_res"), 1)
                if live(s, 0, NC):
                    after(pe, "e_hdm", c.c + 1)
                    project(psum[1], wq, TAB_Q, hdm, 1).then_inc(sem("e_q"), 1)
                    after(pe, "e_km", c.c + 1)
                    for r in range(R):
                        ins = pe.matmul(psum[3][:], att_w[:, r], km[:, r], start=(r == 0), stop=(r == R - 1))
                    ins.then_inc(sem("e_rot"), 1)
                    after(pe, "e_vm", c.c + 1)
                    after(pe, "e_pm", c.c)
                    for r in range(R):
                        ins = pe.matmul(psum[4][:], msg_w[:, r], vm[:, r], start=(r == 0), stop=(r == R - 1))
                    ins.then_inc(sem("e_msg"), 1)
                    after(pe, "e_prod", c.c + 1)
                    after(pe, "e_te", c.c)
                    pe.matmul(psum[5][:], head_ones[:], prod, start=True, stop=True).then_inc(sem("e_att"), 1)
                if live(s, 1, NC):
                    by_type(psum[7], hot_t[:, p.slot, 1], TAB_G, True, True).then_inc(sem("e_g"), 1)
                    after(pe, "e_nm", p.c + 1)
                    pe.matmul(psum[6][:], ident[:], flat(xd[:, p.slot]), start=True, stop=False, skip_group_check=True)
                    by_type(psum[6], hot_t[:, p.slot, 1], TAB_B, False, True).then_inc(sem("e_xb"), 1)
            edge_steps(pe, edge_body)

        @block.vector
        def _(dve):
            chain = [0]

            def link(ins):
                chain[0] += 1
                ins.then_inc(sem("dve_prep"), 1)
                dve.wait_ge(sem("dve_prep"), chain[0])

            dve.memset(top[:, W:W + 1], 0.0)
            dve.memset(run[:, :, W:W + 1], 0.0)
            dve.memset(dstb[:, 0, 0:1], -1).then_inc(sem("dve_init"), 1)
            dve.wait_ge(sem("index_in"), 16 * 9)
            dve.tensor_copy(rows_f[:], rows_i[:]).then_inc(sem("rows_ready"), 1)
            dve.wait_ge(sem("cols_ps"), 3)
            for k in range(3):
                last = dve.tensor_copy(cols_f[:, k, :], psum[k][:, 0:NT])
            link(last)
            for k in range(2):
                dve.tensor_scalar(index[:, :, k, :], cols_f[:, k, :].rearrange("p (c g) -> p c g", g=G),
                                  0.0, None, ALU.max).then_inc(sem("index_ready"), 1)
            link(dve.tensor_tensor(last_of_run[:], cols_f[:, 1, :], cols_f[:, 2, :], ALU.is_equal))
            dve.scalar_tensor_tensor(index[:, :, 2, :], last_of_run[:].rearrange("p (c g) -> p c g", g=G),
                                     float(SKIP_ROW), cols_f[:, 1, :].rearrange("p (c g) -> p c g", g=G),
                                     ALU.mult, ALU.add).then_inc(sem("index_ready"), 1)
            dve.wait_ge(sem("gate_exp"), 2)
            link(dve.tensor_scalar(gate[:, 1, :], gate[:, 1, :], 1.0, None, ALU.add))
            link(dve.reciprocal(gate[:, 2, :], gate[:, 1, :]))
            link(dve.tensor_scalar(gate[:, 3, :], gate[:, 2, :], -1.0, 1.0, ALU.mult, ALU.add))
            link(dve.tensor_scalar(gate_row[:, 1:2], gate_row[:, 1:2], 1.0, None, ALU.add))
            link(dve.reciprocal(gate_row[:, 2:3], gate_row[:, 1:2]))
            dve.wait_ge(sem("types_in"), 32)
            dve.wait_ge(sem("hot_cleared"), 2)

            def one_hot(hot, types, n):
                v = hot.rearrange("p n (k c) -> p n k c", c=32)
                for t in range(T):
                    ins = dve.tensor_scalar(v[:, :, :, t], types.unsqueeze(2).to_broadcast([P, n, 3]),
                                            float(t), None, ALU.is_equal)
                return ins

            def kept(out_ap, types, tmp_sem, base):
                dve.tensor_scalar(out_ap, types, 0.0, gate[:, 3, 0:1], ALU.is_equal, ALU.mult).then_inc(sem(tmp_sem), 1)
                after(dve, tmp_sem, base + 1)

            one_hot(hot_n, nt_all[:], NB * G).then_inc(sem("hot_n_ready"), 1)
            v = hot_n.rearrange("p n (k c) -> p n k c", c=32)
            dve.wait_ge(sem("hot_n_ready"), 1)
            link(dve.tensor_scalar(keep_n[:], v[:, :, 0, 0], gate[:, 3, 0:1], None, ALU.mult))
            link(dve.scalar_tensor_tensor(keep_n[:], v[:, :, 0, 1], gate[:, 3, 1:2], keep_n[:], ALU.mult, ALU.add))
            dve.scalar_tensor_tensor(keep_n[:], v[:, :, 0, 2], gate[:, 3, 2:3], keep_n[:], ALU.mult, ALU.add)\
                .then_inc(sem("keep_ready"), 1)
            dve.wait_ge(sem("weights_in"), W_LOADS)
            link(dve.tensor_scalar(tab[:, TAB_A, :], tab[:, TAB_A, :], gate_row[:, 2:3], None, ALU.mult))
            link(dve.tensor_copy(tab_hi[:], tab[:]))
            link(dve.tensor_tensor(tab_r1[:], tab[:], tab_hi[:], ALU.subtract))
            link(dve.tensor_copy(tab_mid[:], tab_r1[:]))
            link(dve.tensor_tensor(tab_r2[:], tab_r1[:], tab_mid[:], ALU.subtract))
            link(dve.tensor_copy(tab_lo[:], tab_r2[:]))
            for part, t in enumerate((tab_hi, tab_mid, tab_lo)):
                rows = slice(32 * part, 32 * part + 32)
                dve.tensor_copy(tab16[rows], t[rows])
            dve.wait_ge(sem("const"), 5)
            dve.scalar_tensor_tensor(spread_type[:], type_of_row[:], float(T - 1), type_of_row[:],
                                     ALU.is_le, ALU.mult)
            for r in range(R):
                dve.tensor_scalar(att_w[:, r], att_w[:, r], pri[:, r:r + 1], 1.0 / math.sqrt(DK),
                                  ALU.mult, ALU.mult)
            for t in range(T):
                ins = dve.tensor_scalar(wa[:, t], wa[:, t], gate[:, 2, t:t + 1], None, ALU.mult)
            ins.then_inc(sem("tables_ready"), 1)

            def stats(rows, n, b, mv, name, count):
                for g in range(n):
                    ins = dve.bn_stats(b[:, g], rows(g))
                ins.then_inc(sem(name + "_parts"), 1)
                after(dve, name + "_parts", count + 1)
                hold(dve, "dve_turns")
                for g in range(n):
                    ins = dve.bn_aggr(mv[:, g], b[:, g])
                ins.then_inc(sem(name), 1)

            def node_body(s):
                if live(s, 0, NB):
                    after(dve, f"x_in{s.slot}", 16 * (s.round + 1))
                    after(dve, "n_mv1", s.c)
                    stats(lambda g: xa[:, s.slot, g], G, bst, mv1[:, s.slot], "n_mv1", s.c)
                if live(s, 1, NB):
                    p = s.back(1)
                    after(dve, "n_res", p.c + 1)
                    after(dve, "n_mv2", p.c)
                    stats(lambda g: psum[p.slot % 2][:, g * P:(g + 1) * P], G, bst2, mv2[:, p.slot], "n_mv2", p.c)
                if live(s, 2, NB):
                    p = s.back(2)
                    par = p.slot % 2
                    after(dve, "n_nm", p.c + 1)
                    after(dve, "n_g", p.c + 1)
                    after(dve, "n_out", p.c)
                    dve.tensor_tensor(flat(yg[:]), flat(nm[:]), psum[2 + par][:], ALU.mult).then_inc(sem("n_y"), 1)
                    after(dve, "n_y", p.c + 1)
                    after(dve, "n_xb", p.c + 1)
                    after(dve, f"o_out{p.slot}", 16 * p.round)
                    dve.tensor_tensor(flat(oa[:, p.slot]), flat(yg[:]), psum[4 + par][:], ALU.add).then_inc(sem("n_out"), 1)
            node_steps(dve, node_body)

            def mask(out_ap, types, value, rows):
                return dve.scalar_tensor_tensor(out_ap, types, float(value), rows, ALU.is_equal, ALU.mult)

            def edge_body(s):
                c, p = s, s.back(1)
                if live(s, 1, NC):
                    dve.tensor_copy(top[:, 0:1], top[:, W:W + 1]).then_inc(sem("e_top0"), 1)
                    after(dve, "e_top0", p.c + 1)
                    after(dve, "e_cut", p.c + 1)
                    after(dve, "e_att", p.c + 1)
                    dve.tensor_tensor_scan(top[:, 1:W + 1], cut[:, p.slot], psum[5][:], top[:, 0:1],
                                           ALU.add, ALU.max).then_inc(sem("e_top"), 1)
                    after(dve, "e_top", p.c + 1)
                    dve.tensor_tensor(tA, top[:, 0:W], cut[:, p.slot], ALU.add).then_inc(sem("e_tA"), 1)
                    dve.tensor_tensor(te[:, 1], psum[5][:], top[:, 1:W + 1], ALU.subtract)
                    after(dve, "e_tA", p.c + 1)
                    dve.tensor_tensor(te[:, 0], tA, top[:, 1:W + 1], ALU.subtract).then_inc(sem("e_te"), 1)
                if live(s, 0, NC):
                    after(dve, f"g_src{c.slot}", 16 * 2 * G * (c.round + 1))
                    after(dve, f"g_dst{c.slot}", 16 * 2 * G * (c.round + 1))
                    after(dve, "e_turned", c.c)
                    for k in range(2):
                        one_hot(hot_e[:, k], tys[:, c.slot, k], G).then_inc(sem("e_hot16"), 1)
                    after(dve, "e_hot16", 2 * (c.c + 1))
                    hv = hot_e[:, 1].rearrange("p n (k c) -> p n k c", c=32)
                    ke = keep_e[:, c.slot]
                    dve.tensor_scalar(ke, hv[:, :, 0, 0], gate[:, 3, 0:1], None, ALU.mult).then_inc(sem("e_keep"), 1)
                    after(dve, "e_keep", 2 * c.c + 1)
                    dve.scalar_tensor_tensor(ke, hv[:, :, 0, 1], gate[:, 3, 1:2], ke, ALU.mult, ALU.add).then_inc(sem("e_keep"), 1)
                    after(dve, "e_keep", 2 * c.c + 2)
                    dve.scalar_tensor_tensor(ke, hv[:, :, 0, 2], gate[:, 3, 2:3], ke, ALU.mult, ALU.add)
                    after(dve, "e_mv1", c.c)
                    stats(lambda g: (xs if g < G else xd)[:, c.slot, g % G], 2 * G, bst, mv1[:, c.slot], "e_mv1", c.c)
                if live(s, 1, NC):
                    dve.tensor_copy(run[:, :, 0:1], run[:, :, W:W + 1]).then_inc(sem("e_run0"), 1)
                    after(dve, "e_ce", p.c + 1)
                    after(dve, "e_msg", p.c + 1)
                    dve.tensor_tensor(pm, psum[4][:], ce[:, 1], ALU.mult).then_inc(sem("e_pm"), 1)
                    after(dve, "e_run0", p.c + 1)
                    dve.tensor_tensor_scan(run[:, 1, 1:W + 1], ce[:, 0], ce[:, 1], run[:, 1, 0:1],
                                           ALU.mult, ALU.add).then_inc(sem("e_wsum"), 1)
                    after(dve, "e_wsum", p.c + 1)
                    after(dve, "e_lnd", p.c)
                    dve.tensor_scalar(den, run[:, 1, 1:W + 1], DEN_EPS, None, ALU.add).then_inc(sem("e_den"), 1)
                    after(dve, "e_pm", p.c + 1)
                    dve.tensor_tensor_scan(run[:, 0, 1:W + 1], ce[:, 0], pm, run[:, 0, 0:1],
                                           ALU.mult, ALU.add).then_inc(sem("e_run"), 1)
                if live(s, 0, NC):
                    after(dve, f"e_in{c.slot}", 32 * (c.round + 1))
                    after(dve, "e_cut", c.c)
                    dve.tensor_tensor(same[:], dstb[:, c.slot, 1:W + 1], dstb[:, c.slot, 0:W],
                                      ALU.is_equal).then_inc(sem("e_same"), 1)
                if live(s, 1, NC):
                    after(dve, "e_inv0", p.c + 1)
                    dve.tensor_tensor(nt1, den, inv0, ALU.mult).then_inc(sem("e_nt"), 1)
                    after(dve, "e_nt", 2 * p.c + 1)
                    dve.scalar_tensor_tensor(nt2, nt1, 2.0, inv0, ALU.subtract, ALU.mult).then_inc(sem("e_nt"), 1)
                    after(dve, "e_nt", 2 * p.c + 2)
                    after(dve, "e_run", p.c + 1)
                    after(dve, "e_ge", p.c)
                    dve.scalar_tensor_tensor(ag, nt2, -1.0, run[:, 0, 1:W + 1], ALU.mult, ALU.mult)\
                        .then_inc(sem("e_ag"), 1)
                if live(s, 0, NC):
                    after(dve, "e_turned", c.c + 1)
                    after(dve, "e_tyb", 2 * (c.c + 1))
                    for t in range(T):
                        ins = mask(hsm[:, t], tyb[:, c.slot, 0], t, psum[0][:])
                    ins.then_inc(sem("e_hsm"), 1)
                    for t in range(T):
                        ins = mask(hdm[:, t], tyb[:, c.slot, 1], t, psum[1][:])
                    ins.then_inc(sem("e_hdm"), 1)
                if live(s, 1, NC):
                    after(dve, "e_ge", p.c + 1)
                    for t in range(T):
                        ins = mask(gm[:, t], tyb[:, p.slot, 1], t, ge)
                    ins.then_inc(sem("e_gm"), 1)
                if live(s, 0, NC):
                    after(dve, "e_k", c.c + 1)
                    for r in range(R):
                        ins = mask(km[:, r], etb[:, c.slot], r, psum[0][:])
                    ins.then_inc(sem("e_km"), 1)
                    after(dve, "e_v", c.c + 1)
                    for r in range(R):
                        ins = mask(vm[:, r], etb[:, c.slot], r, psum[2][:])
                    ins.then_inc(sem("e_vm"), 1)
                if live(s, 1, NC):
                    after(dve, "e_res", p.c + 1)
                    after(dve, "e_mv2", p.c)
                    stats(lambda g: psum[6][:, g * P:(g + 1) * P], G, bst2, mv2[:, p.slot], "e_mv2", p.c)
                if live(s, 0, NC):
                    after(dve, "e_rot", c.c + 1)
                    after(dve, "e_qs", c.c + 1)
                    dve.tensor_tensor(prod, psum[3][:], qs, ALU.mult).then_inc(sem("e_prod"), 1)
                if live(s, 1, NC):
                    after(dve, "e_nm", p.c + 1)
                    after(dve, "e_g", p.c + 1)
                    dve.tensor_tensor(flat(yge), flat(nme), psum[7][:], ALU.mult).then_inc(sem("e_y"), 1)
                    after(dve, "e_y", p.c + 1)
                    after(dve, "e_xb", p.c + 1)
                    after(dve, f"scattered{p.slot}", 16 * G * p.round)
                    dve.tensor_tensor(flat(oe[:, p.slot]), flat(yge), psum[6][:], ALU.add).then_inc(sem("e_out"), 1)
            dve.wait_ge(sem("nodes_stored"), 1)
            edge_steps(dve, edge_body)


W_LOADS = 16 * (4 + 1 + 3 * 7 + 3 * 8)

_INS = ["x", "src", "dst", "edge_type_4", "node_type_3"] + [
    "L0_gnn_" + n for n in ("Wk", "bk", "Wq", "bq", "Wv", "bv", "Wa", "ba", "rel_pri", "rel_att",
                            "rel_msg", "skip", "ln_g", "ln_b")]


def kernel(**inputs):
    import numpy as np
    import concourse.bacc as bacc
    from concourse.bass_utils import run_bass_kernel_spmd

    nc = bacc.Bacc("TRN2", target_bir_lowering=False, num_devices=1)
    arrays, args = {}, []
    for name in _INS:
        a = np.ascontiguousarray(inputs[name])
        arrays["in_" + name] = a
        args.append(nc.dram_tensor("in_" + name, a.shape, mybir.dt.from_np(a.dtype), kind="ExternalInput").ap())
    shape = inputs["x"].shape
    args.append(nc.dram_tensor("out_x", shape, F32, kind="ExternalOutput").ap())
    gnn_layer(nc, *args)
    r = run_bass_kernel_spmd(nc, [arrays], core_ids=[0])
    return r.results[0]["out_x"]
```

```python
import math

import concourse.bass as bass
from concourse import mybir
from contextlib import ExitStack

F32 = mybir.dt.float32
BF16 = mybir.dt.bfloat16
I32 = mybir.dt.int32
ALU = mybir.AluOpType
ACT = mybir.ActivationFunctionType

P = 128
G = 4
W = P * G
LN_EPS = 1e-05
DEN_EPS = 1e-16
FAR = 1e30
EXP_LN_SET = 6
SKIP_ROW = 1 << 16
TAB = 96


class Step:

    def __init__(self, first, ring, trip=0):
        self.first, self.ring, self.trip = first, ring, trip
        self.c = first + ring * trip
        self.slot = first % ring
        self.round = first // ring + trip

    def back(self, k):
        return Step(self.first - k, self.ring, self.trip)


def gnn_layer(nc, x, src, dst, etype, ntype, Wk, bk, Wq, bq, Wv, bv, Wa, ba,
              rel_pri, rel_att, rel_msg, skip, ln_g, ln_b, table, out):
    N, D = x.shape
    E = src.shape[0]
    T = Wk.shape[0]
    R, H, DK, _ = rel_att.shape
    ROW = table.shape[1]
    assert D == P and H * DK == D
    C_TYPE, C_RSTD, C_BIAS, C_RSTD_KEEP, C_BIAS_KEEP = range(D, D + 5)
    assert ROW >= D + 5
    NG = 2 * G
    NW = P * NG
    NB = -(-N // NW)
    NC = -(-E // W)
    NT = NC * G
    E_LAST = E - (NC - 1) * W
    LO = min(NT, P)
    HI = NT - LO
    FULL = E // P
    REST = E - FULL * P
    RING = 4

    ctx = ExitStack()
    with ctx:
        def sb(name, shape, dt=F32):
            return ctx.enter_context(nc.sbuf_tensor(name, shape, dt))

        sems = {}

        def sem(name):
            if name not in sems:
                sems[name] = ctx.enter_context(nc.semaphore(name))
            return sems[name]

        wk, wq, wv, wa = (sb(n, [P, T, D]) for n in ("wk", "wq", "wv", "wa"))
        att_w = sb("att_w", [P, R, D])
        msg_w = sb("msg_w", [P, R, D])
        pri = sb("pri", [P, R])
        ident = sb("ident", [P, P])
        ident16 = sb("ident16", [P, P], BF16)
        head_ones = sb("head_ones", [P, P])
        NTAB = 6
        tab = sb("tab", [TAB, NTAB, D])
        tab16 = sb("tab16", [TAB, NTAB, D], BF16)
        type_of_row = sb("type_of_row", [TAB, P])
        spread_type = sb("spread_type", [TAB, P], BF16)
        gate_row = sb("gate_row", [TAB, 3])
        gate = sb("gate", [P, 4, T])
        minus_half = sb("minus_half", [P, NG])
        den_eps = sb("den_eps", [P, 1])

        rows_i = sb("rows_i", [P, 2, 3, P], I32)
        cols_f = sb("cols_f", [P, 3, NT])
        last_of_run = sb("last_of_run", [P, NT])
        index = sb("index", [P, NC, 3, G], I32)

        arena = sb("arena", [P, NB * NG * TAB // 2])
        hot_n = arena[:].bitcast(BF16).rearrange("p (n t) -> p n t", t=TAB)
        carved = [0]

        def carve(n):
            k = carved[0]
            carved[0] += n
            assert carved[0] * W <= arena.shape[1]
            v = arena[:, k * W:(k + n) * W]
            return v if n == 1 else v.rearrange("p (n w) -> p n w", w=W)

        hsm, hdm = carve(T), carve(T)
        km, vm = carve(R), carve(R)
        gm = carve(T)
        qs, prod = carve(1), carve(1)
        from_left = carve(1)
        te, ce = carve(2), carve(2)
        pm = carve(1)
        lnd, inv0, nt1, nt2 = (carve(1) for _ in range(4))
        ag, ge, nme, yge = (carve(1) for _ in range(4))
        hd_keep = carve(1)

        rows = sb("rows", [P, RING * NG * ROW])
        xa = rows[:].rearrange("p (s g d) -> p s g d", s=RING, g=NG)
        xd = rows[:, 0:RING * G * ROW].rearrange("p (s g d) -> p s g d", s=RING, g=G)
        xs = rows[:, RING * G * ROW:(RING + 2) * G * ROW].rearrange("p (s g d) -> p s g d", s=2, g=G)
        done_rows = sb("done_rows", [P, 2 * NG * D])
        oa = done_rows[:].rearrange("p (s g d) -> p s g d", s=2, g=NG)
        oe = done_rows[:].rearrange("p (s g d) -> p s g d", s=RING, g=G)
        tab_r1, tab_r2 = (done_rows[0:TAB, k * NTAB * D:(k + 1) * NTAB * D].rearrange("p (n d) -> p n d", n=NTAB)
                          for k in range(2))

        nt_all = sb("nt_all", [P, NB * NG], I32)
        keep_n = sb("keep_n", [P, NB * NG])
        bst = sb("bst", [P, NG, 6])
        bst2 = sb("bst2", [P, NG, 6])
        mv1 = sb("mv1", [P, NG, 2])
        mv2 = sb("mv2", [P, NG, 2])
        sc1 = sb("sc1", [P, 2, NG])
        sc2 = sb("sc2", [P, 2, 4, NG])
        hc = sb("hc", [P, 2, NG, D])
        hot_t = sb("hot_t", [TAB, RING, 2, W], BF16)
        nm = sb("nm", [P, NG, D])
        rows_f = nm[:].rearrange("p g d -> p (g d)")[:, 0:6 * P].rearrange("p (a k e) -> p a k e", a=2, k=3)
        tab_hi, tab_mid = (hc[0:TAB, k].rearrange("p g d -> p (g d)")[:, 0:NTAB * D // 2].bitcast(BF16)
                           .rearrange("p (n d) -> p n d", n=NTAB) for k in range(2))
        tab_lo = nm[0:TAB].rearrange("p g d -> p (g d)")[:, 0:NTAB * D // 2].bitcast(BF16)\
            .rearrange("p (n d) -> p n d", n=NTAB)

        icur = sb("icur", [P, 2, 2, G], I32)
        scur = sb("scur", [P, RING, G], I32)
        hot_e = sb("hot_e", [P, 2, G, TAB], BF16)
        hs = sb("hs", [P, G, D])
        hd = sb("hd", [P, G, D])
        tyb_s = sb("tyb_s", [P, W], BF16)
        tyb_d = sb("tyb_d", [P, RING, W], BF16)
        etb = sb("etb", [P, 2, W], I32)
        dstb = sb("dstb", [P, 2, W + 1], I32)
        same = sb("same", [P, W])
        cut = sb("cut", [P, 2, W])
        top = sb("top", [P, W + 1])
        run = sb("run", [P, 2, W + 1])
        yge2 = sb("yge2", [P, 2, W])

        psum = [ctx.enter_context(nc.psum_tensor(f"bank{i}", [P, W], F32)) for i in range(8)]
        RES_BANKS = ((psum[0], psum[1]), (psum[4], psum[5]))
        block = ctx.enter_context(nc.Block())

        def after(eng, name, value):
            if not isinstance(value, int) or value > 0:
                eng.wait_ge(sem(name), value)

        def hold(eng, name):
            eng.sem_inc(sem(name), 1)

        HEAD = 2 * RING

        def steps(eng, body, n, depth):
            trips = (n - 2 - HEAD) // RING
            for j in range(HEAD):
                body(Step(j, RING))
            with eng.Fori(0, trips) as i:
                for u in range(RING):
                    body(Step(HEAD + u, RING, i))
            for j in range(HEAD + trips * RING, n + depth):
                body(Step(j, RING))

        def node_steps(eng, body):
            steps(eng, body, NB, 2)

        def edge_steps(eng, body):
            steps(eng, body, NC, 3)

        def live(s, k, n):
            return not isinstance(s.c, int) or 0 <= s.c - k < n

        def flat(t):
            return t.rearrange("p g d -> p (g d)")

        TAB_A, TAB_G, TAB_B, TAB_K, TAB_V, TAB_Q = range(NTAB)

        @block.sync
        def _(sp):
            w = sem("weights_in")
            sp.wait_ge(sem("cleared"), 6)
            for k, (v, shift) in enumerate(((src, 0), (dst, 0), (dst, 1))):
                sp.dma_start(rows_i[0:LO, 0, k, :],
                             v[shift:shift + LO * P].rearrange("(t e) -> t e", e=P)).then_inc(sem("index_in"), 16)
                n = FULL - LO if REST or not shift else FULL - LO - 1
                sp.dma_start(rows_i[0:n, 1, k, :],
                             v[shift + LO * P:shift + (LO + n) * P].rearrange("(t e) -> t e", e=P))\
                    .then_inc(sem("index_in"), 16)
                tail = v[shift + (LO + n) * P:E]
                sp.dma_start(rows_i[n:n + 1, 1, k, 0:tail.shape[0]],
                             tail.rearrange("(t e) -> t e", t=1)).then_inc(sem("index_in"), 16)
            sp.dma_start(nt_all[:, (NB - 1) * NG:], ntype[N - NW:N].rearrange("(p j) -> p j", j=NG))\
                .then_inc(sem("types_in"), 16)
            sp.dma_start(nt_all[:, 0:(NB - 1) * NG].rearrange("p (b j) -> p b j", j=NG),
                         ntype[0:(NB - 1) * NW].rearrange("(b p j) -> p b j", p=P, j=NG)).then_inc(sem("types_in"), 16)

            def load_x(base, s):
                sp.dma_start(xa[:, s.slot, :, 0:D], x[bass.ds(base, NW), :].rearrange("(p j) d -> p j d", j=NG))\
                    .then_inc(sem(f"x_in{s.slot}"), 16)

            ahead = 2
            for b in range(ahead):
                load_x(b * NW, Step(b, RING))
            for dst_w, src_w in ((wk, Wk), (wq, Wq), (wv, Wv), (wa, Wa)):
                sp.dma_start(dst_w[:, :, :], src_w.rearrange("t i o -> i t o")).then_inc(w, 16)
            sp.dma_start(gate[:, 0, :], skip.rearrange("(a t) -> a t", a=1).to_broadcast([P, T])).then_inc(w, 16)
            for part in range(3):
                for k, v in enumerate((ba, ln_g, ln_b, bk, bv, bq)):
                    sp.dma_start(tab[32 * part:32 * part + T, k, :], v).then_inc(w, 16)
                sp.dma_start(gate_row[32 * part:32 * part + T, 0:1],
                             skip.rearrange("(t a) -> t a", a=1)).then_inc(w, 16)
            for h in range(H):
                hrows = slice(h * DK, (h + 1) * DK)
                sp.dma_start(att_w[hrows, :, hrows], rel_att[:, h].rearrange("r d f -> d r f")).then_inc(w, 16)
                sp.dma_start(msg_w[hrows, :, hrows], rel_msg[:, h].rearrange("r d f -> d r f")).then_inc(w, 16)
                sp.dma_start(pri[hrows, :],
                             rel_pri[:, h:h + 1].rearrange("r a -> a r").to_broadcast([DK, R]),
                             allow_slow_non_contiguous=True).then_inc(w, 16)

            def store(name, rows_out, sbuf, base, slot):
                sp.dma_start(rows_out[bass.ds(base, NW), :].rearrange("(p j) d -> p j d", j=NG), sbuf)\
                    .then_inc(sem(f"{name}{slot}"), 16)

            def node_body(s):
                if live(s, 0, NB):
                    after(sp, "n_sc1", s.c + 1)
                    after(sp, "n_type", s.c + 1)
                    last = isinstance(s.c, int) and s.c == NB - 1
                    if last:
                        q = s.back(1)
                        sp.wait_ge(sem(f"t_out{q.slot}"), 16 * (q.round + 1))
                    store("t_out", table, xa[:, s.slot], N - NW if last else s.c * NW, s.slot)
                if live(s, -ahead, NB):
                    f = s.back(-ahead)
                    after(sp, "n_xb", 2 * (f.c - RING + 1))
                    after(sp, f"t_out{f.slot}", 16 * f.round)
                    load_x(min(f.c * NW, N - NW) if isinstance(f.c, int) else f.c * NW, f)
                if live(s, 2, NB):
                    p = s.back(2)
                    after(sp, "n_out", 2 * (p.c + 1))
                    last = isinstance(p.c, int) and p.c == NB - 1
                    if last:
                        q = p.back(1)
                        sp.wait_ge(sem(f"o_out{q.slot % 2}"), 16 * len(range(q.slot % 2, q.c + 1, 2)))
                    store("o_out", out, oa[:, p.slot % 2], N - NW if last else p.c * NW, p.slot % 2)

            node_steps(sp, node_body)
            for slot in range(2):
                sp.wait_ge(sem(f"o_out{slot}"), 16 * len(range(slot, NB, 2)))
            for slot in range(RING):
                sp.wait_ge(sem(f"t_out{slot}"), 16 * len(range(slot, NB, RING)))
            sp.sem_inc(sem("nodes_stored"), 1)

            def edge_body(s):
                if not live(s, 0, NC):
                    return
                after(sp, "e_vm", s.c - 1)
                after(sp, "e_same", s.c - 1)
                at = s.slot % 2
                n = E_LAST if isinstance(s.c, int) and s.c == NC - 1 else W
                sp.dma_start(etb[:, at, 0:n],
                             etype[bass.ds(s.c * W, n)].rearrange("(a e) -> a e", a=1).to_broadcast([P, n]))\
                    .then_inc(sem(f"e_in{s.slot}"), 16)
                lead = 0 if isinstance(s.c, int) and s.c == 0 else 1
                if not lead:
                    sp.wait_ge(sem("dve_init"), 1)
                sp.dma_start(dstb[:, at, 1 - lead:n + 1],
                             dst[bass.ds(s.c * W - lead, n + lead)].rearrange("(a e) -> a e", a=1)
                             .to_broadcast([P, n + lead])).then_inc(sem(f"e_in{s.slot}"), 16)
            edge_steps(sp, edge_body)

        @block.gpsimd
        def _(pool):
            for t in (rows_i, tab, att_w, msg_w):
                pool.memset(t[:], 0 if t is not rows_i else -1).then_inc(sem("cleared"), 1)
            pool.memset(gate_row[:], 0.0).then_inc(sem("cleared"), 1)
            pool.memset(xa[:, :, :, D + 5:ROW], 0.0).then_inc(sem("cleared"), 1)
            pool.memset(minus_half[:], -0.5).then_inc(sem("const"), 1)
            pool.memset(den_eps[:], DEN_EPS).then_inc(sem("const"), 1)
            for t in (ident, ident16):
                pool.memset(t[:], 0.0).then_inc(sem("pool_prep"), 1)
            pool.memset(head_ones[:], 1.0).then_inc(sem("pool_prep"), 1)
            pool.wait_ge(sem("pool_prep"), 3)
            for t in (ident, ident16):
                pool.affine_select(out=t[:], in_=t[:], compare_op=ALU.not_equal, fill=1.0, base=0,
                                   pattern=[[-1, P]], channel_multiplier=1).then_inc(sem("const"), 1)
            ho = head_ones[:].rearrange("p (h d) -> p h d", d=DK)
            pool.affine_select(out=ho, in_=ho, compare_op=ALU.is_ge, fill=0.0, base=0,
                               pattern=[[-DK, H], [0, DK]], channel_multiplier=1).then_inc(sem("pool_prep"), 1)
            pool.wait_ge(sem("pool_prep"), 4)
            pool.affine_select(out=ho, in_=ho, compare_op=ALU.is_ge, fill=0.0, base=DK - 1,
                               pattern=[[DK, H], [0, DK]], channel_multiplier=-1).then_inc(sem("const"), 1)
            pool.iota(type_of_row[:], pattern=[[0, P]], base=0, channel_multiplier=1,
                      allow_small_or_imprecise_dtypes=True).then_inc(sem("const"), 1)

            def linker(name, base):
                k = [0]

                def link(ins):
                    k[0] += 1
                    ins.then_inc(sem(name), 1)
                    after(pool, name, base + k[0])
                    hold(pool, "pool_turns")
                return link

            def norm1(s):
                col = lambda c: xa[:, s.slot, :, c]
                keep = keep_n[:, bass.ds(s.c * NG, NG)]
                link = linker("pool_n1", 4 * s.c)
                link(pool.tensor_scalar(sc1[:, 0], mv1[:, :, 1], LN_EPS, None, ALU.add))
                link(pool.tensor_tensor(col(C_RSTD), sc1[:, 0], minus_half[:], ALU.pow))
                pool.tensor_tensor(col(C_RSTD_KEEP), col(C_RSTD), keep, ALU.mult)
                link(pool.tensor_tensor(sc1[:, 1], mv1[:, :, 0], col(C_RSTD), ALU.mult))
                link(pool.tensor_scalar(col(C_BIAS), sc1[:, 1], -1.0, None, ALU.mult))
                pool.tensor_tensor(col(C_BIAS_KEEP), col(C_BIAS), keep, ALU.mult).then_inc(sem("n_sc1"), 1)

            def norm2(s, n, mv, sc, link, done):
                link(pool.tensor_scalar(sc[:, 0, 0:n], mv[:, 0:n, 1], LN_EPS, None, ALU.add))
                link(pool.tensor_tensor(sc[:, 1, 0:n], sc[:, 0, 0:n], minus_half[:, 0:n], ALU.pow))
                link(pool.tensor_tensor(sc[:, 2, 0:n], mv[:, 0:n, 0], sc[:, 1, 0:n], ALU.mult))
                pool.tensor_scalar(sc[:, 3, 0:n], sc[:, 2, 0:n], -1.0, None, ALU.mult).then_inc(sem(done), 1)

            pool.wait_ge(sem("keep_ready"), 1)

            def node_body(s):
                if live(s, 0, NB):
                    after(pool, "n_mv1", s.c + 1)
                    hold(pool, "pool_turns")
                    norm1(s)
                if live(s, 1, NB):
                    p = s.back(1)
                    after(pool, "n_mv2", p.c + 1)
                    hold(pool, "pool_turns")
                    norm2(p, NG, mv2, sc2[:, p.slot % 2], linker("pool_n2", 3 * p.c), "n_sc2")
            node_steps(pool, node_body)

            pool.wait_ge(sem("index_ready"), 3)

            def gathers(s, k):
                for g in range(G):
                    pool.indirect_dma_start(
                        out=xd[:, s.slot, g, :] if k else xs[:, s.slot % 2, g, :], out_offset=None, in_=table,
                        in_offset=bass.IndirectOffsetOnAxis(ap=icur[:, s.slot % 2, k, g:g + 1], axis=0))\
                        .then_inc(sem(f"g_{'sd'[k]}{s.slot}"), 16)

            def gather_indices(s):
                chunk = index[:, s.c, 0:2, :] if isinstance(s.c, int) else \
                    index[:, bass.ds(s.c, 1), 0:2, :].rearrange("p a k g -> p (a k) g")
                if not isinstance(s.c, int) or s.c >= 2:
                    q = s.back(2)
                    for k in "sd":
                        after(pool, f"g_{k}{q.slot}", 16 * G * (q.round + 1))
                    hold(pool, "pool_turns")
                pool.tensor_copy(icur[:, s.slot % 2], chunk).then_inc(sem("icur_ready"), 1)
                after(pool, "icur_ready", s.c + 1)
                hold(pool, "pool_turns")

            pool.wait_ge(sem("nodes_stored"), 1)
            gather_indices(Step(0, RING))
            gathers(Step(0, RING), 0)
            gathers(Step(0, RING), 1)

            def edge_body(s):
                n = s.back(-1)
                if live(s, 3, NC):
                    p = s.back(3)
                    after(pool, "e_mv2", p.c + 1)
                    hold(pool, "pool_turns")
                    norm2(p, G, mv2, sc2[:, p.slot % 2], linker("pool_e2", 3 * p.c), "e_sc2")
                if live(s, -1, NC):
                    gather_indices(n)
                    after(pool, "e_turned", n.c - 1)
                    hold(pool, "pool_turns")
                    gathers(n, 0)
                if live(s, 3, NC):
                    after(pool, f"scattered{p.slot}", 16 * G * p.round)
                    after(pool, "e_y2", p.c + 1)
                    hold(pool, "pool_turns")
                    pool.tensor_tensor(oe[:, p.slot], xd[:, p.slot, :, 0:D],
                                       yge2[:, p.slot % 2].rearrange("p (g d) -> p g d", g=G), ALU.add)\
                        .then_inc(sem("e_out"), 1)
                    pool.tensor_copy(scur[:, p.slot], index[:, p.c, 2, :] if isinstance(p.c, int) else
                                     index[:, bass.ds(p.c, 1), 2, :].rearrange("p a g -> p (a g)"))\
                        .then_inc(sem("scur_ready"), 1)
                    after(pool, "e_out", p.c + 1)
                    after(pool, "scur_ready", p.c + 1)
                    hold(pool, "pool_turns")
                if live(s, -1, NC):
                    gathers(n, 1)
                if live(s, 3, NC):
                    for g in range(G):
                        pool.indirect_dma_start(
                            out=out, out_offset=bass.IndirectOffsetOnAxis(ap=scur[:, p.slot, g:g + 1], axis=0),
                            in_=oe[:, p.slot, g, :], in_offset=None, bounds_check=N - 1, oob_is_err=False)\
                            .then_inc(sem(f"scattered{p.slot}"), 16)
            edge_steps(pool, edge_body)
            for slot in range(RING):
                pool.wait_ge(sem(f"scattered{slot}"), 16 * G * len(range(slot, NC, RING)))

        @block.scalar
        def _(act):
            act.wait_ge(sem("weights_in"), W_LOADS)
            act.activation(gate[:, 1, :], gate[:, 0, :], ACT.Exp, scale=-1.0).then_inc(sem("gate_exp"), 1)
            act.activation(gate_row[:, 1:2], gate_row[:, 0:1], ACT.Exp, scale=-1.0).then_inc(sem("gate_exp"), 1)

            def node_body(s):
                if live(s, 0, NB):
                    after(act, f"x_in{s.slot}", 16 * (s.round + 1))
                    after(act, "n_sc1", s.c + 1)
                    after(act, "n_res", 2 * (s.c - 1))
                    for h in range(2):
                        for g in range(h * G, (h + 1) * G):
                            row = xa[:, s.slot, g]
                            ins = act.activation(hc[:, s.slot % 2, g], row[:, 0:D], ACT.Relu,
                                                 bias=row[:, C_BIAS_KEEP:C_BIAS_KEEP + 1],
                                                 scale=row[:, C_RSTD_KEEP:C_RSTD_KEEP + 1])
                        ins.then_inc(sem("n_hc"), 1)
                    after(act, "n_hot_ps", s.c + 1)
                    act.activation(hot_t[:, s.slot], psum[6][0:TAB, :].bitcast(BF16).rearrange("p (k e) -> p k e", k=2),
                                   ACT.Copy).then_inc(sem("n_hot"), 1)
                if live(s, 1, NB):
                    p = s.back(1)
                    after(act, "n_sc2", p.c + 1)
                    after(act, "n_res", 2 * (p.c + 1))
                    after(act, "n_out", 2 * p.c)
                    res = RES_BANKS[p.slot % 2]
                    for g in range(NG):
                        ins = act.activation(nm[:, g], res[g // G][:, g % G * P:(g % G + 1) * P], ACT.Identity,
                                             bias=sc2[:, p.slot % 2, 3, g:g + 1], scale=sc2[:, p.slot % 2, 1, g:g + 1])
                    ins.then_inc(sem("n_nm"), 1)
            node_steps(act, node_body)

            def edge_body(s):
                c, b, a, z = s, s.back(1), s.back(2), s.back(3)
                if live(s, 2, NC):
                    act.add_instruction(mybir.InstLoadActFuncSet(
                        name=nc.get_next_instruction_name(), act_func_set_id=EXP_LN_SET, ins=[], outs=[]))
                    after(act, "e_te", a.c + 1)
                    act.activation(flat(ce), flat(te), ACT.Exp).then_inc(sem("e_ce"), 1)
                if live(s, 0, NC):
                    after(act, f"g_s{c.slot}", 16 * G * (c.round + 1))
                    after(act, f"g_d{c.slot}", 16 * G * (c.round + 1))
                    after(act, "e_turned", c.c)
                    for g in range(G):
                        for to, row in ((hs, xs[:, c.slot % 2, g]), (hd, xd[:, c.slot, g])):
                            ins = act.activation(to[:, g], row[:, 0:D], ACT.Relu, bias=row[:, C_BIAS:C_BIAS + 1],
                                                 scale=row[:, C_RSTD:C_RSTD + 1])
                    ins.then_inc(sem("e_h"), 1)
                if live(s, 3, NC):
                    after(act, "e_sc2", z.c + 1)
                    after(act, "e_res", z.c + 1)
                    for g in range(G):
                        ins = act.activation(nme[:, g * D:(g + 1) * D], psum[6][:, g * P:(g + 1) * P], ACT.Identity,
                                             bias=sc2[:, z.slot % 2, 3, g:g + 1], scale=sc2[:, z.slot % 2, 1, g:g + 1])
                    ins.then_inc(sem("e_nm"), 1)
                if live(s, 1, NC):
                    after(act, "e_q", b.c + 1)
                    act.activation(qs, psum[5][:], ACT.Copy).then_inc(sem("e_qs"), 1)
                if live(s, 0, NC):
                    after(act, "e_turned", c.c + 1)
                    act.activation(hot_t[:, c.slot], psum[2][0:TAB, :].bitcast(BF16).rearrange("p (k e) -> p k e", k=2),
                                   ACT.Copy).then_inc(sem("e_hot"), 1)
                if live(s, 2, NC):
                    after(act, "e_wsum", a.c + 1)
                    act.activation(lnd, run[:, 1, 1:W + 1], ACT.Ln, bias=den_eps[:]).then_inc(sem("e_lnd"), 1)
                    after(act, "e_lnd", a.c + 1)
                    act.activation(inv0, lnd, ACT.Exp, scale=-1.0).then_inc(sem("e_inv0"), 1)
                if live(s, 1, NC):
                    after(act, "e_same", b.c + 1)
                    act.activation(cut[:, b.slot % 2], same[:], ACT.Copy, bias=-FAR, scale=FAR).then_inc(sem("e_cut"), 1)
                if live(s, 0, NC):
                    after(act, "e_spread", 2 * (c.c + 1))
                    act.activation(tyb_s[:], psum[2][:], ACT.Copy).then_inc(sem("e_tyb"), 1)
                    act.activation(tyb_d[:, c.slot], psum[5][:], ACT.Copy).then_inc(sem("e_tyb"), 1)
                if live(s, 2, NC):
                    after(act, "e_ag", a.c + 1)
                    act.activation(ge, ag, ACT.Gelu).then_inc(sem("e_ge"), 1)
                    after(act, "e_res", a.c)
                    for g in range(G):
                        row = xd[:, a.slot, g]
                        ins = act.activation(hd_keep[:, g * D:(g + 1) * D], row[:, 0:D], ACT.Relu,
                                             bias=row[:, C_BIAS_KEEP:C_BIAS_KEEP + 1],
                                             scale=row[:, C_RSTD_KEEP:C_RSTD_KEEP + 1])
                    ins.then_inc(sem("e_hc"), 1)
            edge_steps(act, edge_body)

        @block.tensor
        def _(pe):
            pe.wait_ge(sem("const"), 6)
            pe.wait_ge(sem("rows_ready"), 1)
            for k in range(3):
                pe.transpose(psum[k][:, 0:LO], rows_f[0:LO, 0, k, :], ident[0:LO, 0:LO])
                pe.transpose(psum[k][:, LO:NT], rows_f[0:HI, 1, k, :], ident[0:HI, 0:HI])\
                    .then_inc(sem("cols_ps"), 1)
            pe.wait_ge(sem("tables_ready"), 1)
            pe.wait_ge(sem("index_ready"), 3)
            pe.wait_ge(sem("hot_n_ready"), 1)

            def by_type(ps, hot, tab_row, start, stop):
                for g in range(G):
                    ins = pe.matmul(ps[:, g * P:(g + 1) * P], hot[:, g * P:(g + 1) * P], tab16[:, tab_row, :],
                                    start=start, stop=stop, skip_group_check=True)
                return ins

            def node_body(s):
                if live(s, 1, NB):
                    p = s.back(1)
                    after(pe, "n_hot", p.c + 1)
                    after(pe, "n_nm", p.c - 1)
                    for h, res in enumerate(RES_BANKS[p.slot % 2]):
                        after(pe, "n_hc", 2 * p.c + h + 1)
                        pe.matmul(res[:], ident[:], flat(hc[:, p.slot % 2, h * G:(h + 1) * G]),
                                  start=True, stop=False, skip_group_check=True)
                        by_type(res, hot_t[:, p.slot, h], TAB_A, False, True).then_inc(sem("n_res"), 1)
                if live(s, 2, NB):
                    p = s.back(2)
                    after(pe, "n_out", 2 * p.c)
                    for h in range(2):
                        by_type(psum[2 + h], hot_t[:, p.slot, h], TAB_G, True, True).then_inc(sem("n_g"), 1)
                    for h, bank in enumerate((7, 2)):
                        if h:
                            after(pe, "n_y", 2 * p.c + 1)
                        pe.matmul(psum[bank][:], ident[:], xa[:, p.slot, h * G:(h + 1) * G, 0:D],
                                  start=True, stop=False, skip_group_check=True)
                        by_type(psum[bank], hot_t[:, p.slot, h], TAB_B, False, True).then_inc(sem("n_xb"), 1)
                if live(s, 0, NB):
                    after(pe, "n_hot", s.c)
                    ps = psum[6][0:TAB, :].bitcast(BF16)
                    for g in range(NG):
                        ins = pe.transpose(ps[:, g * P:(g + 1) * P],
                                           hot_n[:, bass.ds(s.c * NG + g, 1), :].rearrange("p a t -> p (a t)"),
                                           ident16[:])
                    ins.then_inc(sem("n_hot_ps"), 1)
            node_steps(pe, node_body)
            pe.wait_ge(sem("n_out"), 2 * NB)

            def project(ps, weights, tab_row, rows_m, hot, s):
                for t in range(T):
                    pe.matmul(ps[:], weights[:, t], rows_m[:, t], start=(t == 0), stop=False)
                return pe.matmul(ps[:], tab16[:, tab_row, :], hot, start=False, stop=True)

            def edge_body(s):
                c, b, a, z = s, s.back(1), s.back(2), s.back(3)
                if live(s, 1, NC):
                    after(pe, "e_hsm", b.c + 1)
                    after(pe, "e_prod", b.c)
                    project(psum[3], wk, TAB_K, hsm, hot_t[:, b.slot, 0], b).then_inc(sem("e_k"), 1)
                if live(s, 3, NC):
                    after(pe, "e_y", z.c)
                    by_type(psum[7], hot_t[:, z.slot, 1], TAB_G, True, True).then_inc(sem("e_g"), 1)
                if live(s, 1, NC):
                    after(pe, "e_hdm", b.c + 1)
                    after(pe, "e_te1", b.c)
                    project(psum[5], wq, TAB_Q, hdm, hot_t[:, b.slot, 1], b).then_inc(sem("e_q"), 1)
                if live(s, 0, NC):
                    after(pe, "e_h", c.c + 1)
                    after(pe, "e_hsm", c.c)
                    after(pe, "e_hdm", c.c)
                    for g in range(G):
                        pe.transpose(psum[0][:, g * P:(g + 1) * P], hs[:, g], ident[:])
                        pe.transpose(psum[1][:, g * P:(g + 1) * P], hd[:, g], ident[:])
                    after(pe, "e_hot16", 2 * (c.c + 1))
                    after(pe, "e_tyb", 2 * c.c)
                    for k in range(2):
                        for g in range(G):
                            ins = pe.transpose(psum[2][0:TAB, :].bitcast(BF16)[:, k * W + g * P:k * W + (g + 1) * P],
                                               hot_e[:, k, g, :], ident16[:])
                    ins.then_inc(sem("e_turned"), 1)
                if live(s, 3, NC):
                    after(pe, "e_nm", z.c + 1)
                    by_type(psum[6], hot_t[:, z.slot, 1], TAB_B, True, True).then_inc(sem("e_b"), 1)
                if live(s, 1, NC):
                    after(pe, "e_pm", b.c)
                    project(psum[4], wv, TAB_V, hsm, hot_t[:, b.slot, 0], b).then_inc(sem("e_v"), 1)
                if live(s, 0, NC):
                    after(pe, "e_hot", c.c + 1)
                    pe.matmul(psum[2][:], spread_type[:], hot_t[:, c.slot, 0], start=True, stop=True)\
                        .then_inc(sem("e_spread"), 1)
                    after(pe, "e_qs", c.c)
                    pe.matmul(psum[5][:], spread_type[:], hot_t[:, c.slot, 1], start=True, stop=True)\
                        .then_inc(sem("e_spread"), 1)
                if live(s, 1, NC):
                    after(pe, "e_km", b.c + 1)
                    for r in range(R):
                        ins = pe.matmul(psum[3][:], att_w[:, r], km[:, r], start=(r == 0), stop=(r == R - 1))
                    ins.then_inc(sem("e_rot"), 1)
                    after(pe, "e_vm", b.c + 1)
                    for r in range(R):
                        ins = pe.matmul(psum[4][:], msg_w[:, r], vm[:, r], start=(r == 0), stop=(r == R - 1))
                    ins.then_inc(sem("e_msg"), 1)
                    after(pe, "e_prod", b.c + 1)
                    after(pe, "e_tyb", 2 * (min(b.c + 2, NC) if isinstance(b.c, int) else b.c + 2))
                    pe.matmul(psum[5][:], head_ones[:], prod, start=True, stop=True).then_inc(sem("e_att"), 1)
                if live(s, 2, NC):
                    after(pe, "e_hc", a.c + 1)
                    after(pe, "e_y2", a.c)
                    pe.matmul(psum[6][:], ident[:], hd_keep, start=True, stop=False, skip_group_check=True)
                    after(pe, "e_gm", a.c + 1)
                    for t in range(T):
                        for g in range(G):
                            pe.matmul(psum[6][:, g * P:(g + 1) * P], gm[:, t, g * P:(g + 1) * P], wa[:, t],
                                      start=False, stop=False, skip_group_check=True)
                    by_type(psum[6], hot_t[:, a.slot, 1], TAB_A, False, True).then_inc(sem("e_res"), 1)
            edge_steps(pe, edge_body)

        @block.vector
        def _(dve):
            chain = [0]

            def link(ins):
                chain[0] += 1
                ins.then_inc(sem("dve_prep"), 1)
                dve.wait_ge(sem("dve_prep"), chain[0])

            dve.memset(top[:, W:W + 1], 0.0)
            dve.memset(run[:, :, W:W + 1], 0.0)
            dve.memset(hot_e[:].rearrange("p k g t -> p (k g t)").bitcast(F32), 0.0)
            dve.memset(dstb[:, 0, 0:1], -1).then_inc(sem("dve_init"), 1)
            link(dve.memset(arena[:], 0.0))
            dve.wait_ge(sem("index_in"), 16 * 9)
            dve.tensor_copy(rows_f, rows_i[:]).then_inc(sem("rows_ready"), 1)

            def one_hot(hot, types, n):
                v = hot.rearrange("p n (k c) -> p n k c", c=32)
                for t in range(T):
                    ins = dve.tensor_scalar(v[:, :, :, t], types.unsqueeze(2).to_broadcast([P, n, 3]),
                                            float(t), None, ALU.is_equal)
                return ins

            dve.wait_ge(sem("types_in"), 32)
            one_hot(hot_n, nt_all[:], NB * NG).then_inc(sem("hot_n_ready"), 1)
            dve.wait_ge(sem("cols_ps"), 3)
            for k in range(3):
                last = dve.tensor_copy(cols_f[:, k, :], psum[k][:, 0:NT])
            link(last)
            for k in range(2):
                dve.tensor_scalar(index[:, :, k, :], cols_f[:, k, :].rearrange("p (c g) -> p c g", g=G),
                                  0.0, None, ALU.max).then_inc(sem("index_ready"), 1)
            link(dve.tensor_tensor(last_of_run[:], cols_f[:, 1, :], cols_f[:, 2, :], ALU.is_equal))
            dve.scalar_tensor_tensor(index[:, :, 2, :], last_of_run[:].rearrange("p (c g) -> p c g", g=G),
                                     float(SKIP_ROW), cols_f[:, 1, :].rearrange("p (c g) -> p c g", g=G),
                                     ALU.mult, ALU.add).then_inc(sem("index_ready"), 1)
            dve.wait_ge(sem("gate_exp"), 2)
            link(dve.tensor_scalar(gate[:, 1, :], gate[:, 1, :], 1.0, None, ALU.add))
            link(dve.reciprocal(gate[:, 2, :], gate[:, 1, :]))
            link(dve.tensor_scalar(gate[:, 3, :], gate[:, 2, :], -1.0, 1.0, ALU.mult, ALU.add))
            link(dve.tensor_scalar(gate_row[:, 1:2], gate_row[:, 1:2], 1.0, None, ALU.add))
            link(dve.reciprocal(gate_row[:, 2:3], gate_row[:, 1:2]))
            v = hot_n.rearrange("p n (k c) -> p n k c", c=32)
            dve.wait_ge(sem("hot_n_ready"), 1)
            link(dve.tensor_scalar(keep_n[:], v[:, :, 0, 0], gate[:, 3, 0:1], None, ALU.mult))
            link(dve.scalar_tensor_tensor(keep_n[:], v[:, :, 0, 1], gate[:, 3, 1:2], keep_n[:], ALU.mult, ALU.add))
            dve.scalar_tensor_tensor(keep_n[:], v[:, :, 0, 2], gate[:, 3, 2:3], keep_n[:], ALU.mult, ALU.add)\
                .then_inc(sem("keep_ready"), 1)
            dve.wait_ge(sem("weights_in"), W_LOADS)
            dve.wait_ge(sem("cols_ps"), 3)
            link(dve.tensor_scalar(tab[:, TAB_A, :], tab[:, TAB_A, :], gate_row[:, 2:3], None, ALU.mult))
            link(dve.tensor_copy(tab_hi, tab[:]))
            link(dve.tensor_tensor(tab_r1, tab[:], tab_hi, ALU.subtract))
            link(dve.tensor_copy(tab_mid, tab_r1))
            link(dve.tensor_tensor(tab_r2, tab_r1, tab_mid, ALU.subtract))
            link(dve.tensor_copy(tab_lo, tab_r2))
            for part, t in enumerate((tab_hi, tab_mid, tab_lo)):
                part_rows = slice(32 * part, 32 * part + 32)
                dve.tensor_copy(tab16[part_rows], t[part_rows])
            dve.wait_ge(sem("const"), 6)
            dve.scalar_tensor_tensor(spread_type[:], type_of_row[:], float(T - 1), type_of_row[:],
                                     ALU.is_le, ALU.mult)
            for r in range(R):
                dve.tensor_scalar(att_w[:, r], att_w[:, r], pri[:, r:r + 1], 1.0 / math.sqrt(DK),
                                  ALU.mult, ALU.mult)
            for t in range(T):
                ins = dve.tensor_scalar(wa[:, t], wa[:, t], gate[:, 2, t:t + 1], None, ALU.mult)
            ins.then_inc(sem("tables_ready"), 1)
            dve.wait_ge(sem("tables_ready"), 1)

            def stats(rows_of, n, b, mv, name, count, ready=None):
                for g in range(n):
                    if ready:
                        ready(g)
                    ins = dve.bn_stats(b[:, g], rows_of(g))
                ins.then_inc(sem(name + "_parts"), 1)
                after(dve, name + "_parts", count + 1)
                hold(dve, "dve_turns")
                for g in range(n):
                    ins = dve.bn_aggr(mv[:, g], b[:, g])
                ins.then_inc(sem(name), 1)

            def node_body(s):
                if live(s, 0, NB):
                    after(dve, f"x_in{s.slot}", 16 * (s.round + 1))
                    after(dve, "n_sc1", s.c)
                    dve.tensor_copy(xa[:, s.slot, :, C_TYPE], nt_all[:, bass.ds(s.c * NG, NG)]).then_inc(sem("n_type"), 1)
                    stats(lambda g: xa[:, s.slot, g, 0:D], NG, bst, mv1, "n_mv1", s.c)
                if live(s, 1, NB):
                    p = s.back(1)
                    after(dve, "n_sc2", p.c)
                    res = RES_BANKS[p.slot % 2]
                    stats(lambda g: res[g // G][:, g % G * P:(g % G + 1) * P], NG, bst2, mv2, "n_mv2", p.c,
                          lambda g: after(dve, "n_res", 2 * p.c + g // G + 1) if g % G == 0 else None)
                if live(s, 2, NB):
                    p = s.back(2)
                    after(dve, "n_nm", p.c + 1)
                    halves = [flat(nm[:, h * G:(h + 1) * G]) for h in range(2)]
                    for h in range(2):
                        after(dve, "n_g", 2 * p.c + h + 1)
                        dve.tensor_tensor(halves[h], halves[h], psum[2 + h][:], ALU.mult).then_inc(sem("n_y"), 1)
                    after(dve, f"o_out{p.slot % 2}", 16 * (2 * p.round + p.slot // 2))
                    for h, bank in enumerate((7, 2)):
                        after(dve, "n_y", 2 * p.c + h + 1)
                        after(dve, "n_xb", 2 * p.c + h + 1)
                        dve.tensor_tensor(flat(oa[:, p.slot % 2, h * G:(h + 1) * G]), halves[h], psum[bank][:],
                                          ALU.add).then_inc(sem("n_out"), 1)
            node_steps(dve, node_body)

            def mask(out_ap, types, value, rows_in):
                return dve.scalar_tensor_tensor(out_ap, types, float(value), rows_in, ALU.is_equal, ALU.mult)

            def edge_body(s):
                c, b, a, z = s, s.back(1), s.back(2), s.back(3)
                if live(s, 2, NC):
                    dve.tensor_copy(top[:, 0:1], top[:, W:W + 1]).then_inc(sem("e_top0"), 1)
                    after(dve, "e_top0", a.c + 1)
                    after(dve, "e_cut", a.c + 1)
                    after(dve, "e_att", a.c + 1)
                    at = a.slot % 2
                    dve.tensor_tensor_scan(top[:, 1:W + 1], cut[:, at], psum[5][:], top[:, 0:1],
                                           ALU.add, ALU.max).then_inc(sem("e_top"), 1)
                    after(dve, "e_top", a.c + 1)
                    dve.tensor_tensor(te[:, 1], psum[5][:], top[:, 1:W + 1], ALU.subtract).then_inc(sem("e_te1"), 1)
                    dve.tensor_tensor(from_left, top[:, 0:W], cut[:, at], ALU.add).then_inc(sem("e_left"), 1)
                    after(dve, "e_left", a.c + 1)
                    dve.tensor_tensor(te[:, 0], from_left, top[:, 1:W + 1], ALU.subtract).then_inc(sem("e_te"), 1)
                if live(s, 1, NC):
                    after(dve, "e_turned", b.c + 1)
                    after(dve, "e_tyb", 2 * (b.c + 1))
                    after(dve, "e_q", b.c)
                    for t in range(T):
                        ins = mask(hdm[:, t], tyb_d[:, b.slot], t, psum[1][:])
                    ins.then_inc(sem("e_hdm"), 1)
                if live(s, 3, NC):
                    after(dve, "e_res", z.c + 1)
                    stats(lambda g: psum[6][:, g * P:(g + 1) * P], G, bst2, mv2, "e_mv2", z.c)
                if live(s, 0, NC):
                    after(dve, f"g_s{c.slot}", 16 * G * (c.round + 1))
                    after(dve, f"g_d{c.slot}", 16 * G * (c.round + 1))
                    for k, r in enumerate((xs[:, c.slot % 2], xd[:, c.slot])):
                        one_hot(hot_e[:, k], r[:, :, C_TYPE], G).then_inc(sem("e_hot16"), 1)
                if live(s, 1, NC):
                    after(dve, f"e_in{b.slot}", 32 * (b.round + 1))
                    after(dve, "e_cut", b.c)
                    dve.tensor_tensor(same[:], dstb[:, b.slot % 2, 1:W + 1], dstb[:, b.slot % 2, 0:W],
                                      ALU.is_equal).then_inc(sem("e_same"), 1)
                    after(dve, "e_k", b.c + 1)
                    for r in range(R):
                        ins = mask(km[:, r], etb[:, b.slot % 2], r, psum[3][:])
                    ins.then_inc(sem("e_km"), 1)
                if live(s, 2, NC):
                    dve.tensor_copy(run[:, :, 0:1], run[:, :, W:W + 1]).then_inc(sem("e_run0"), 1)
                    after(dve, "e_ce", a.c + 1)
                    after(dve, "e_msg", a.c + 1)
                    dve.tensor_tensor(pm, psum[4][:], ce[:, 1], ALU.mult).then_inc(sem("e_pm"), 1)
                    after(dve, "e_run0", a.c + 1)
                    dve.tensor_tensor_scan(run[:, 1, 1:W + 1], ce[:, 0], ce[:, 1], run[:, 1, 0:1],
                                           ALU.mult, ALU.add).then_inc(sem("e_wsum"), 1)
                    after(dve, "e_pm", a.c + 1)
                    dve.tensor_tensor_scan(run[:, 0, 1:W + 1], ce[:, 0], pm, run[:, 0, 0:1],
                                           ALU.mult, ALU.add).then_inc(sem("e_run"), 1)
                if live(s, 3, NC):
                    after(dve, "e_nm", z.c + 1)
                    after(dve, "e_g", z.c + 1)
                    dve.tensor_tensor(yge, nme, psum[7][:], ALU.mult).then_inc(sem("e_y"), 1)
                    after(dve, "e_y", z.c + 1)
                    after(dve, "e_b", z.c + 1)
                    after(dve, "e_out", z.c - 1)
                    dve.tensor_tensor(yge2[:, z.slot % 2], yge, psum[6][:], ALU.add).then_inc(sem("e_y2"), 1)
                if live(s, 2, NC):
                    after(dve, "e_inv0", a.c + 1)
                    after(dve, "e_wsum", a.c + 1)
                    dve.scalar_tensor_tensor(nt1, run[:, 1, 1:W + 1], DEN_EPS, inv0, ALU.add, ALU.mult)\
                        .then_inc(sem("e_nt"), 1)
                    after(dve, "e_nt", 2 * a.c + 1)
                    dve.scalar_tensor_tensor(nt2, nt1, 2.0, inv0, ALU.subtract, ALU.mult).then_inc(sem("e_nt"), 1)
                    after(dve, "e_nt", 2 * a.c + 2)
                    after(dve, "e_run", a.c + 1)
                    dve.scalar_tensor_tensor(ag, nt2, -1.0, run[:, 0, 1:W + 1], ALU.mult, ALU.mult)\
                        .then_inc(sem("e_ag"), 1)
                if live(s, 1, NC):
                    after(dve, "e_v", b.c + 1)
                    for r in range(R):
                        ins = mask(vm[:, r], etb[:, b.slot % 2], r, psum[4][:])
                    ins.then_inc(sem("e_vm"), 1)
                    after(dve, "e_rot", b.c + 1)
                    after(dve, "e_qs", b.c + 1)
                    dve.tensor_tensor(prod, psum[3][:], qs, ALU.mult).then_inc(sem("e_prod"), 1)
                if live(s, 2, NC):
                    after(dve, "e_ge", a.c + 1)
                    for t in range(T):
                        ins = mask(gm[:, t], tyb_d[:, a.slot], t, ge)
                    ins.then_inc(sem("e_gm"), 1)
                if live(s, 0, NC):
                    after(dve, "e_turned", c.c + 1)
                    after(dve, "e_tyb", 2 * c.c + 1)
                    after(dve, "e_v", c.c)
                    for t in range(T):
                        ins = mask(hsm[:, t], tyb_s[:], t, psum[0][:])
                    ins.then_inc(sem("e_hsm"), 1)
            edge_steps(dve, edge_body)


TABLE_ROW = 136
W_LOADS = 16 * (4 + 1 + 3 * 7 + 3 * 8)

_INS = ["x", "src", "dst", "edge_type_4", "node_type_3"] + [
    "L0_gnn_" + n for n in ("Wk", "bk", "Wq", "bq", "Wv", "bv", "Wa", "ba", "rel_pri", "rel_att",
                            "rel_msg", "skip", "ln_g", "ln_b")]


def kernel(**inputs):
    import numpy as np
    import concourse.bacc as bacc
    from concourse.bass_utils import run_bass_kernel_spmd

    nc = bacc.Bacc("TRN2", target_bir_lowering=False, num_devices=1)
    arrays, args = {}, []
    for name in _INS:
        a = np.ascontiguousarray(inputs[name])
        arrays["in_" + name] = a
        args.append(nc.dram_tensor("in_" + name, a.shape, mybir.dt.from_np(a.dtype), kind="ExternalInput").ap())
    shape = inputs["x"].shape
    args.append(nc.dram_tensor("out_x", shape, F32, kind="ExternalOutput").ap())
    table = nc.dram_tensor("node_table", (shape[0], TABLE_ROW), F32, kind="Internal").ap()
    gnn_layer(nc, *args[:-1], table, args[-1])
    r = run_bass_kernel_spmd(nc, [arrays], core_ids=[0])
    return r.results[0]["out_x"]
```

```python
import math

import concourse.bass as bass
from concourse import mybir
from contextlib import ExitStack

F32 = mybir.dt.float32
BF16 = mybir.dt.bfloat16
I32 = mybir.dt.int32
ALU = mybir.AluOpType
ACT = mybir.ActivationFunctionType

P = 128
G = 4
W = P * G
LN_EPS = 1e-05
DEN_EPS = 1e-16
FAR = 1e30
EXP_LN_SET = 6
SKIP_ROW = 1 << 16
PARTS = 3


class Step:

    def __init__(self, first, ring, trip=0):
        self.first, self.ring, self.trip = first, ring, trip
        self.c = first + ring * trip
        self.slot = first % ring
        self.round = first // ring + trip

    def back(self, k):
        return Step(self.first - k, self.ring, self.trip)


def gnn_layer(nc, x, src, dst, etype, ntype, Wk, bk, Wq, bq, Wv, bv, Wa, ba,
              rel_pri, rel_att, rel_msg, skip, ln_g, ln_b, table, out):
    N, D = x.shape
    E = src.shape[0]
    T = Wk.shape[0]
    R, H, DK, _ = rel_att.shape
    ROW = table.shape[1]
    TAB = PARTS * T
    assert D == P and H * DK == D
    X0 = 8
    XC = slice(X0, X0 + D)
    C_RSTD, C_BIAS, C_RSTD_KEEP, C_BIAS_KEEP = range(X0 + D, X0 + D + 4)
    assert TAB <= 2 * X0 and C_BIAS_KEEP < ROW
    NG = 2 * G
    TURN = NG * TAB
    NW = P * NG
    NB = -(-N // NW)
    NC = -(-E // W)
    NT = NC * G
    E_LAST = E - (NC - 1) * W
    LO = min(NT, P)
    HI = NT - LO
    FULL = E // P
    REST = E - FULL * P
    RING = 4

    ctx = ExitStack()
    with ctx:
        def sb(name, shape, dt=F32):
            return ctx.enter_context(nc.sbuf_tensor(name, shape, dt))

        sems = {}

        def sem(name):
            if name not in sems:
                sems[name] = ctx.enter_context(nc.semaphore(name))
            return sems[name]

        wk, wq, wv, wa = (sb(n, [P, T, D]) for n in ("wk", "wq", "wv", "wa"))
        att_w = sb("att_w", [P, R, D])
        msg_w = sb("msg_w", [P, R, D])
        pri = sb("pri", [P, R])
        att_c, msg_c = (sb(n, [P, R, DK]) for n in ("att_c", "msg_c"))
        ident = sb("ident", [P, P])
        ident16 = sb("ident16", [P, P], BF16)
        head_ones = sb("head_ones", [P, P])
        NTAB = 6
        tab = sb("tab", [TAB, NTAB, D])
        tab16 = sb("tab16", [TAB, NTAB, D], BF16)
        part_mask = sb("part_mask", [TAB, PARTS])
        type_of_row = sb("type_of_row", [TAB, P])
        spread_type = sb("spread_type", [TAB, P], BF16)
        gate_row = sb("gate_row", [TAB, 3])
        gate = sb("gate", [P, 4, T])
        minus_half = sb("minus_half", [P, NG])
        den_eps = sb("den_eps", [P, 1])

        rows_i = sb("rows_i", [P, 2, 3, P], I32)
        cols_f = sb("cols_f", [P, 3, NT])
        last_of_run = sb("last_of_run", [P, NT])
        index = sb("index", [P, NC, 3, G], I32)

        arena = sb("arena", [P, 35 * W])
        hot_flat = arena[:, 0:(NB * NG * TAB + TURN) // 2].bitcast(BF16)
        hot_n = hot_flat[:, 0:NB * NG * TAB].rearrange("p (n t) -> p n t", t=TAB)
        carved = [0]

        def carve(n):
            k = carved[0]
            carved[0] += n
            assert carved[0] * W <= arena.shape[1]
            v = arena[:, k * W:(k + n) * W]
            return v if n == 1 else v.rearrange("p (n w) -> p n w", w=W)

        hsm, hdm = carve(T), carve(T)
        km, vm = carve(R), carve(R)
        gm = carve(T)
        qs, prod = carve(1), carve(1)
        from_left = carve(1)
        te, ce = carve(2), carve(2)
        pm = carve(1)
        lnd, inv0, nt1, nt2 = (carve(1) for _ in range(4))
        ag, ge = carve(1), carve(1)
        hd_keep = carve(1)
        nme, yge = carve(1), carve(1)

        rows = sb("rows", [P, RING * NG * ROW])
        assert (NB - 1) % RING == 0
        rows16 = rows[:].bitcast(BF16)
        xa = rows[:].rearrange("p (s g d) -> p s g d", s=RING, g=NG)
        xa16 = rows16.rearrange("p (s g d) -> p s g d", s=RING, g=NG)
        xs = rows[:, NG * ROW:(NG + 2 * G) * ROW].rearrange("p (s g d) -> p s g d", s=2, g=G)
        xd = rows[:, (NG + 2 * G) * ROW:].rearrange("p (s g d) -> p s g d", s=RING, g=G)
        xs16 = rows16[:, 2 * NG * ROW:2 * (NG + 2 * G) * ROW].rearrange("p (s g d) -> p s g d", s=2, g=G)
        xd16 = rows16[:, 2 * (NG + 2 * G) * ROW:].rearrange("p (s g d) -> p s g d", s=RING, g=G)
        done_rows = sb("done_rows", [P, 2 * NG * D])
        oa = done_rows[:].rearrange("p (s g d) -> p s g d", s=2, g=NG)
        oe = done_rows[:].rearrange("p (s g d) -> p s g d", s=RING, g=G)
        tab_r1, tab_r2 = (done_rows[0:TAB, k * NTAB * D:(k + 1) * NTAB * D].rearrange("p (n d) -> p n d", n=NTAB)
                          for k in range(2))

        nt_all = sb("nt_all", [P, NB * NG], I32)
        keep_n = sb("keep_n", [P, NB * NG])
        bst = sb("bst", [P, NG, 6])
        bst2 = sb("bst2", [P, NG, 6])
        mv1 = sb("mv1", [P, NG, 2])
        mv2 = sb("mv2", [P, NG, 2])
        sc1 = sb("sc1", [P, 3, NG])
        sc2 = sb("sc2", [P, 2, 4, NG])
        hc = sb("hc", [P, 2, NG, D])
        hot_t = sb("hot_t", [TAB, RING, 2, W], BF16)
        nm = sb("nm", [P, NG, D])
        rows_f = nm[:].rearrange("p g d -> p (g d)")[:, 0:6 * P].rearrange("p (a k e) -> p a k e", a=2, k=3)
        tab_hi, tab_mid = (hc[0:TAB, k].rearrange("p g d -> p (g d)")[:, 0:NTAB * D // 2].bitcast(BF16)
                           .rearrange("p (n d) -> p n d", n=NTAB) for k in range(2))
        tab_lo = nm[0:TAB].rearrange("p g d -> p (g d)")[:, 0:NTAB * D // 2].bitcast(BF16)\
            .rearrange("p (n d) -> p n d", n=NTAB)

        icur = sb("icur", [P, 2, 2, G], I32)
        scur = sb("scur", [P, RING, G], I32)
        hs = sb("hs", [P, G, D])
        hd = sb("hd", [P, G, D])
        tyb_s = sb("tyb_s", [P, W], BF16)
        tyb_d = sb("tyb_d", [P, RING, W], BF16)
        etb = sb("etb", [P, 2, W], I32)
        dstb = sb("dstb", [P, 2, W + 1], I32)
        step = sb("step", [P, W], I32)
        cut = sb("cut", [P, 2, W])
        top = sb("top", [P, W + 1])
        run = sb("run", [P, 2, W])
        yge2 = sb("yge2", [P, 2, W])

        psum = [ctx.enter_context(nc.psum_tensor(f"bank{i}", [P, W], F32)) for i in range(8)]
        RES_BANKS = ((psum[0], psum[1]), (psum[4], psum[5]))
        block = ctx.enter_context(nc.Block())

        def after(eng, name, value):
            if not isinstance(value, int) or value > 0:
                eng.wait_ge(sem(name), value)

        def hold(eng, name):
            eng.sem_inc(sem(name), 1)

        W_LOADS = 16 * (4 + 2 + H)

        HEAD = 2 * RING

        def steps(eng, body, n, depth):
            trips = (n - 2 - HEAD) // RING
            for j in range(HEAD):
                body(Step(j, RING))
            with eng.Fori(0, trips) as i:
                for u in range(RING):
                    body(Step(HEAD + u, RING, i))
            for j in range(HEAD + trips * RING, n + depth):
                body(Step(j, RING))

        def node_steps(eng, body):
            steps(eng, body, NB, 2)

        def edge_steps(eng, body):
            steps(eng, body, NC, 3)

        def live(s, k, n):
            return not isinstance(s.c, int) or 0 <= s.c - k < n

        def flat(t):
            return t.rearrange("p g d -> p (g d)")

        TAB_A, TAB_G, TAB_B, TAB_K, TAB_V, TAB_Q = range(NTAB)

        @block.sync
        def _(sp):
            def load_x(base, s):
                sp.dma_start(xa[:, s.slot, :, XC], x[bass.ds(base, NW), :].rearrange("(p j) d -> p j d", j=NG))\
                    .then_inc(sem(f"x_in{s.slot}"), 16)

            sp.dma_start(nt_all[:, (NB - 1) * NG:], ntype[N - NW:N].rearrange("(p j) -> p j", j=NG))\
                .then_inc(sem("types_in"), 16)
            sp.dma_start(nt_all[:, 0:(NB - 1) * NG].rearrange("p (b j) -> p b j", j=NG),
                         ntype[0:(NB - 1) * NW].rearrange("(b p j) -> p b j", p=P, j=NG)).then_inc(sem("types_in"), 16)
            ahead = 2
            load_x(0, Step(0, RING))
            sp.dma_start(gate[:, 0, :], skip.rearrange("(a t) -> a t", a=1).to_broadcast([P, T]))\
                .then_inc(sem("gates_in"), 16)
            for part in range(PARTS):
                sp.dma_start(gate_row[part * T:(part + 1) * T, 0:1], skip.rearrange("(t a) -> t a", a=1))\
                    .then_inc(sem("gates_in"), 16)
            for part in range(PARTS):
                for k, v in enumerate((ba, ln_g, ln_b, bk, bv, bq)):
                    sp.dma_start(tab[part * T:(part + 1) * T, k, :], v).then_inc(sem("tab_in"), 16)
            for b in range(1, ahead):
                load_x(b * NW, Step(b, RING))
            sp.wait_ge(sem("cleared"), 1)
            for k, (v, shift) in enumerate(((src, 0), (dst, 0), (dst, 1))):
                sp.dma_start(rows_i[0:LO, 0, k, :],
                             v[shift:shift + LO * P].rearrange("(t e) -> t e", e=P)).then_inc(sem("index_in"), 16)
                n = FULL - LO if REST or not shift else FULL - LO - 1
                sp.dma_start(rows_i[0:n, 1, k, :],
                             v[shift + LO * P:shift + (LO + n) * P].rearrange("(t e) -> t e", e=P))\
                    .then_inc(sem("index_in"), 16)
                tail = v[shift + (LO + n) * P:E]
                sp.dma_start(rows_i[n:n + 1, 1, k, 0:tail.shape[0]],
                             tail.rearrange("(t e) -> t e", t=1)).then_inc(sem("index_in"), 16)
            w = sem("weights_in")
            for dst_w, src_w in ((wk, Wk), (wq, Wq), (wv, Wv), (wa, Wa)):
                sp.dma_start(dst_w[:, :, :], src_w.rearrange("t i o -> i t o")).then_inc(w, 16)
            for dst_w, src_w in ((att_c, rel_att), (msg_c, rel_msg)):
                sp.dma_start(dst_w[:, :, :], src_w.rearrange("r h d f -> (h d) r f")).then_inc(w, 16)
            for h in range(H):
                sp.dma_start(pri[h * DK:(h + 1) * DK, :],
                             rel_pri[:, h:h + 1].rearrange("r a -> a r").to_broadcast([DK, R]),
                             allow_slow_non_contiguous=True).then_inc(w, 16)

            def store(name, rows_out, sbuf, base, slot):
                sp.dma_start(rows_out[bass.ds(base, NW), :].rearrange("(p j) d -> p j d", j=NG), sbuf)\
                    .then_inc(sem(f"{name}{slot}"), 16)

            def node_body(s):
                if live(s, 0, NB):
                    after(sp, "n_sc1", s.c + 1)
                    after(sp, "n_type", s.c + 1)
                    last = isinstance(s.c, int) and s.c == NB - 1
                    if last:
                        q = s.back(1)
                        sp.wait_ge(sem(f"t_out{q.slot}"), 16 * (q.round + 1))
                    store("t_out", table, xa[:, s.slot], N - NW if last else s.c * NW, s.slot)
                if live(s, -ahead, NB):
                    f = s.back(-ahead)
                    after(sp, "n_xb", 2 * (f.c - RING + 1))
                    after(sp, f"t_out{f.slot}", 16 * f.round)
                    load_x(min(f.c * NW, N - NW) if isinstance(f.c, int) else f.c * NW, f)
                if isinstance(s.c, int) and s.c == NB:
                    for slot in range(RING):
                        sp.wait_ge(sem(f"t_out{slot}"), 16 * len(range(slot, NB, RING)))
                    sp.sem_inc(sem("table_stored"), 1)
                if live(s, 2, NB):
                    p = s.back(2)
                    after(sp, "n_out", 2 * (p.c + 1))
                    last = isinstance(p.c, int) and p.c == NB - 1
                    if last:
                        q = p.back(1)
                        sp.wait_ge(sem(f"o_out{q.slot % 2}"), 16 * len(range(q.slot % 2, q.c + 1, 2)))
                    store("o_out", out, oa[:, p.slot % 2], N - NW if last else p.c * NW, p.slot % 2)

            node_steps(sp, node_body)
            for slot in range(2):
                sp.wait_ge(sem(f"o_out{slot}"), 16 * len(range(slot, NB, 2)))
            sp.sem_inc(sem("nodes_stored"), 1)

            def edge_body(s):
                if not live(s, 0, NC):
                    return
                after(sp, "e_vm", s.c - 1)
                after(sp, "e_step", s.c - 1)
                at = s.slot % 2
                n = E_LAST if isinstance(s.c, int) and s.c == NC - 1 else W
                sp.dma_start(etb[:, at, 0:n],
                             etype[bass.ds(s.c * W, n)].rearrange("(a e) -> a e", a=1).to_broadcast([P, n]))\
                    .then_inc(sem(f"e_in{s.slot}"), 16)
                lead = 0 if isinstance(s.c, int) and s.c == 0 else 1
                if not lead:
                    sp.wait_ge(sem("dve_init"), 1)
                sp.dma_start(dstb[:, at, 1 - lead:n + 1],
                             dst[bass.ds(s.c * W - lead, n + lead)].rearrange("(a e) -> a e", a=1)
                             .to_broadcast([P, n + lead])).then_inc(sem(f"e_in{s.slot}"), 16)
            edge_steps(sp, edge_body)

        @block.gpsimd
        def _(pool):
            pool.memset(rows_i[:], -1).then_inc(sem("cleared"), 1)
            pool.memset(xa[:, :, :, 0:X0], 0.0)
            pool.memset(xa[:, :, :, C_BIAS_KEEP + 1:ROW], 0.0)
            pool.memset(minus_half[:], -0.5).then_inc(sem("const"), 1)
            pool.memset(den_eps[:], DEN_EPS).then_inc(sem("const"), 1)
            for t in (ident, ident16):
                pool.memset(t[:], 0.0).then_inc(sem("pool_prep"), 1)
            pool.memset(head_ones[:], 1.0).then_inc(sem("pool_prep"), 1)
            pool.memset(part_mask[:], 1.0).then_inc(sem("pool_prep"), 1)
            pool.wait_ge(sem("pool_prep"), 4)
            for t in (ident, ident16):
                pool.affine_select(out=t[:], in_=t[:], compare_op=ALU.not_equal, fill=1.0, base=0,
                                   pattern=[[-1, P]], channel_multiplier=1).then_inc(sem("const"), 1)
            ho = head_ones[:].rearrange("p (h d) -> p h d", d=DK)
            pool.affine_select(out=ho, in_=ho, compare_op=ALU.is_ge, fill=0.0, base=0,
                               pattern=[[-DK, H], [0, DK]], channel_multiplier=1).then_inc(sem("pool_prep"), 1)
            pool.affine_select(out=part_mask[:], in_=part_mask[:], compare_op=ALU.is_ge, fill=0.0, base=0,
                               pattern=[[-T, PARTS]], channel_multiplier=1).then_inc(sem("pool_prep"), 1)
            pool.wait_ge(sem("pool_prep"), 6)
            pool.affine_select(out=part_mask[:], in_=part_mask[:], compare_op=ALU.is_ge, fill=0.0, base=T - 1,
                               pattern=[[T, PARTS]], channel_multiplier=-1).then_inc(sem("const"), 1)
            pool.affine_select(out=ho, in_=ho, compare_op=ALU.is_ge, fill=0.0, base=DK - 1,
                               pattern=[[DK, H], [0, DK]], channel_multiplier=-1).then_inc(sem("const"), 1)
            pool.iota(type_of_row[:], pattern=[[0, P]], base=0, channel_multiplier=1,
                      allow_small_or_imprecise_dtypes=True).then_inc(sem("const"), 1)

            def formed(ins, name, count):
                ins.then_inc(sem(name), 1)
                after(pool, name, count)
                hold(pool, "pool_turns")

            def norm1(s):
                col = lambda c: xa[:, s.slot, :, c]
                keep = keep_n[:, bass.ds(s.c * NG, NG)]
                pool.tensor_scalar(sc1[:, 1], mv1[:, :, 0], -1.0, None, ALU.mult)
                formed(pool.tensor_scalar(sc1[:, 0], mv1[:, :, 1], LN_EPS, None, ALU.add), "pool_n1", 2 * s.c + 1)
                pool.tensor_tensor(sc1[:, 2], sc1[:, 1], keep, ALU.mult)
                formed(pool.tensor_tensor(col(C_RSTD), sc1[:, 0], minus_half[:], ALU.pow), "pool_n1", 2 * s.c + 2)
                pool.tensor_tensor(col(C_RSTD_KEEP), col(C_RSTD), keep, ALU.mult)
                pool.tensor_tensor(col(C_BIAS), sc1[:, 1], col(C_RSTD), ALU.mult)
                pool.tensor_tensor(col(C_BIAS_KEEP), sc1[:, 2], col(C_RSTD), ALU.mult).then_inc(sem("n_sc1"), 1)

            def norm2(s, n, mv, sc, name, done):
                pool.tensor_scalar(sc[:, 2, 0:n], mv[:, 0:n, 0], -1.0, None, ALU.mult)
                formed(pool.tensor_scalar(sc[:, 0, 0:n], mv[:, 0:n, 1], LN_EPS, None, ALU.add), name, 2 * s.c + 1)
                formed(pool.tensor_tensor(sc[:, 1, 0:n], sc[:, 0, 0:n], minus_half[:, 0:n], ALU.pow), name, 2 * s.c + 2)
                pool.tensor_tensor(sc[:, 3, 0:n], sc[:, 2, 0:n], sc[:, 1, 0:n], ALU.mult).then_inc(sem(done), 1)

            def gathers(s, k):
                for g in range(G):
                    pool.indirect_dma_start(
                        out=xd[:, s.slot, g, :] if k else xs[:, s.slot % 2, g, :], out_offset=None, in_=table,
                        in_offset=bass.IndirectOffsetOnAxis(ap=icur[:, s.slot % 2, k, g:g + 1], axis=0))\
                        .then_inc(sem(f"g_{'sd'[k]}{s.slot}"), 16)

            def gather_indices(s):
                chunk = index[:, s.c, 0:2, :] if isinstance(s.c, int) else \
                    index[:, bass.ds(s.c, 1), 0:2, :].rearrange("p a k g -> p (a k) g")
                if not isinstance(s.c, int) or s.c >= 2:
                    q = s.back(2)
                    for k in "sd":
                        after(pool, f"g_{k}{q.slot}", 16 * G * (q.round + 1))
                    hold(pool, "pool_turns")
                pool.tensor_copy(icur[:, s.slot % 2], chunk).then_inc(sem("icur_ready"), 1)
                after(pool, "icur_ready", s.c + 1)
                hold(pool, "pool_turns")

            pool.wait_ge(sem("keep_ready"), 1)

            def node_body(s):
                if isinstance(s.c, int) and s.c == NB:
                    pool.wait_ge(sem("index_ready"), 3)
                    pool.wait_ge(sem("table_stored"), 1)
                    pool.wait_ge(sem("n_xb"), 2 * (NB - 3))
                    gather_indices(Step(0, RING))
                    gathers(Step(0, RING), 0)
                if live(s, 0, NB):
                    after(pool, "n_mv1", s.c + 1)
                    hold(pool, "pool_turns")
                    norm1(s)
                if live(s, 1, NB):
                    p = s.back(1)
                    after(pool, "n_mv2", p.c + 1)
                    hold(pool, "pool_turns")
                    norm2(p, NG, mv2, sc2[:, p.slot % 2], "pool_n2", "n_sc2")
            node_steps(pool, node_body)

            pool.wait_ge(sem("n_xb"), 2 * (NB - 1))
            gathers(Step(0, RING), 1)

            def edge_body(s):
                n = s.back(-1)
                if live(s, 2, NC):
                    a = s.back(2)
                    after(pool, "e_top", a.c + 1)
                    hold(pool, "pool_turns")
                    pool.tensor_tensor(from_left, top[:, 0:W], cut[:, a.slot % 2], ALU.add).then_inc(sem("e_left"), 1)
                if live(s, 3, NC):
                    p = s.back(3)
                    after(pool, "e_mv2", p.c + 1)
                    hold(pool, "pool_turns")
                    norm2(p, G, mv2, sc2[:, p.slot % 2], "pool_e2", "e_sc2")
                if live(s, 1, NC):
                    b = s.back(1)
                    after(pool, f"e_in{b.slot}", 32 * (b.round + 1))
                    after(pool, "e_cut", b.c)
                    hold(pool, "pool_turns")
                    pool.tensor_tensor(step[:], dstb[:, b.slot % 2, 1:W + 1], dstb[:, b.slot % 2, 0:W],
                                       ALU.subtract).then_inc(sem("e_step"), 1)
                if live(s, -1, NC):
                    gather_indices(n)
                    after(pool, "e_turned", n.c - 1)
                    hold(pool, "pool_turns")
                    gathers(n, 0)
                if live(s, 3, NC):
                    after(pool, f"scattered{p.slot}", 16 * G * p.round)
                    after(pool, "e_y2", p.c + 1)
                    hold(pool, "pool_turns")
                    pool.tensor_tensor(oe[:, p.slot], xd[:, p.slot, :, XC],
                                       yge2[:, p.slot % 2].rearrange("p (g d) -> p g d", g=G), ALU.add)\
                        .then_inc(sem("e_out"), 1)
                    pool.tensor_copy(scur[:, p.slot], index[:, p.c, 2, :] if isinstance(p.c, int) else
                                     index[:, bass.ds(p.c, 1), 2, :].rearrange("p a g -> p (a g)"))\
                        .then_inc(sem("scur_ready"), 1)
                    after(pool, "e_out", p.c + 1)
                    after(pool, "scur_ready", p.c + 1)
                    hold(pool, "pool_turns")
                if live(s, -1, NC):
                    gathers(n, 1)
                if live(s, 3, NC):
                    if isinstance(p.c, int) and p.c == 0:
                        pool.wait_ge(sem("nodes_stored"), 1)
                    for g in range(G):
                        pool.indirect_dma_start(
                            out=out, out_offset=bass.IndirectOffsetOnAxis(ap=scur[:, p.slot, g:g + 1], axis=0),
                            in_=oe[:, p.slot, g, :], in_offset=None, bounds_check=N - 1, oob_is_err=False)\
                            .then_inc(sem(f"scattered{p.slot}"), 16)
            edge_steps(pool, edge_body)
            for slot in range(RING):
                pool.wait_ge(sem(f"scattered{slot}"), 16 * G * len(range(slot, NC, RING)))

        @block.scalar
        def _(act):
            act.wait_ge(sem("gates_in"), 16 * (1 + PARTS))
            act.activation(gate[:, 1, :], gate[:, 0, :], ACT.Exp, scale=-1.0).then_inc(sem("gate_exp"), 1)
            act.activation(gate_row[:, 1:2], gate_row[:, 0:1], ACT.Exp, scale=-1.0).then_inc(sem("gate_exp"), 1)

            def keep_hot(s):
                after(act, "n_hot_ps", s.c + 1)
                act.activation(hot_t[:, s.slot], psum[3][0:TAB, :].bitcast(BF16).rearrange("p (k e) -> p k e", k=2),
                               ACT.Copy).then_inc(sem("n_hot"), 1)

            def node_body(s):
                if live(s, 0, NB):
                    after(act, f"x_in{s.slot}", 16 * (s.round + 1))
                    after(act, "n_sc1", s.c + 1)
                    after(act, "n_res", 2 * (s.c - 1))
                    for h in range(2):
                        for g in range(h * G, (h + 1) * G):
                            row = xa[:, s.slot, g]
                            ins = act.activation(hc[:, s.slot % 2, g], row[:, XC], ACT.Relu,
                                                 bias=row[:, C_BIAS_KEEP:C_BIAS_KEEP + 1],
                                                 scale=row[:, C_RSTD_KEEP:C_RSTD_KEEP + 1])
                        ins.then_inc(sem("n_hc"), 1)
                if live(s, -1, NB):
                    keep_hot(s.back(-1))
                if live(s, 1, NB):
                    p = s.back(1)
                    after(act, "n_sc2", p.c + 1)
                    after(act, "n_res", 2 * (p.c + 1))
                    after(act, "n_out", 2 * p.c)
                    res = RES_BANKS[p.slot % 2]
                    for g in range(NG):
                        ins = act.activation(nm[:, g], res[g // G][:, g % G * P:(g % G + 1) * P], ACT.Identity,
                                             bias=sc2[:, p.slot % 2, 3, g:g + 1], scale=sc2[:, p.slot % 2, 1, g:g + 1])
                    ins.then_inc(sem("n_nm"), 1)
            keep_hot(Step(0, RING))
            node_steps(act, node_body)

            def edge_body(s):
                c, b, a, z = s, s.back(1), s.back(2), s.back(3)
                if live(s, 2, NC):
                    act.add_instruction(mybir.InstLoadActFuncSet(
                        name=nc.get_next_instruction_name(), act_func_set_id=EXP_LN_SET, ins=[], outs=[]))
                    after(act, "e_te", a.c + 1)
                    act.activation(flat(ce), flat(te), ACT.Exp).then_inc(sem("e_ce"), 1)
                if live(s, 0, NC):
                    after(act, f"g_s{c.slot}", 16 * G * (c.round + 1))
                    after(act, f"g_d{c.slot}", 16 * G * (c.round + 1))
                    after(act, "e_turned", c.c)
                    for g in range(G):
                        for to, row in ((hs, xs[:, c.slot % 2, g]), (hd, xd[:, c.slot, g])):
                            ins = act.activation(to[:, g], row[:, XC], ACT.Relu, bias=row[:, C_BIAS:C_BIAS + 1],
                                                 scale=row[:, C_RSTD:C_RSTD + 1])
                    ins.then_inc(sem("e_h"), 1)
                if live(s, 3, NC):
                    after(act, "e_sc2", z.c + 1)
                    after(act, "e_y", z.c)
                    for g in range(G):
                        ins = act.activation(nme[:, g * D:(g + 1) * D], hd_keep[:, g * P:(g + 1) * P], ACT.Identity,
                                             bias=sc2[:, z.slot % 2, 3, g:g + 1], scale=sc2[:, z.slot % 2, 1, g:g + 1])
                    ins.then_inc(sem("e_nm"), 1)
                if live(s, 2, NC):
                    after(act, "e_wsum", a.c + 1)
                    act.activation(lnd, run[:, 1], ACT.Ln, bias=den_eps[:]).then_inc(sem("e_lnd"), 1)
                    after(act, "e_lnd", a.c + 1)
                    act.activation(inv0, lnd, ACT.Exp, scale=-1.0).then_inc(sem("e_inv0"), 1)
                if live(s, 0, NC):
                    after(act, "e_turned", c.c + 1)
                    act.activation(hot_t[:, c.slot], psum[2][0:TAB, :].bitcast(BF16).rearrange("p (k e) -> p k e", k=2),
                                   ACT.Copy).then_inc(sem("e_hot"), 1)
                if live(s, 1, NC):
                    after(act, "e_q", b.c + 1)
                    act.activation(qs, psum[5][:], ACT.Copy).then_inc(sem("e_qs"), 1)
                if live(s, 1, NC):
                    after(act, "e_step", b.c + 1)
                    act.activation(cut[:, b.slot % 2], step[:], ACT.Copy, scale=-FAR).then_inc(sem("e_cut"), 1)
                if live(s, 0, NC):
                    after(act, "e_spread", 2 * (c.c + 1))
                    act.activation(tyb_s[:], psum[2][:], ACT.Copy).then_inc(sem("e_tyb"), 1)
                    act.activation(tyb_d[:, c.slot], psum[5][:], ACT.Copy).then_inc(sem("e_tyb"), 1)
                if live(s, 2, NC):
                    after(act, "e_ag", a.c + 1)
                    act.activation(ge, ag, ACT.Gelu).then_inc(sem("e_ge"), 1)
                    for g in range(G):
                        row = xd[:, a.slot, g]
                        ins = act.activation(hd_keep[:, g * D:(g + 1) * D], row[:, XC], ACT.Relu,
                                             bias=row[:, C_BIAS_KEEP:C_BIAS_KEEP + 1],
                                             scale=row[:, C_RSTD_KEEP:C_RSTD_KEEP + 1])
                    ins.then_inc(sem("e_hc"), 1)
            edge_steps(act, edge_body)

        @block.tensor
        def _(pe):
            pe.wait_ge(sem("const"), 7)
            pe.wait_ge(sem("tables_ready"), 1)
            pe.wait_ge(sem("hot_n_ready"), 1)

            def by_type(ps, hot, tab_row, start, stop):
                for g in range(G):
                    ins = pe.matmul(ps[:, g * P:(g + 1) * P], hot[:, g * P:(g + 1) * P], tab16[:, tab_row, :],
                                    start=start, stop=stop, skip_group_check=True)
                return ins

            def turn_hot(s):
                after(pe, "n_hot", s.c)
                ps = psum[3][0:TURN, :].bitcast(BF16)
                for g in range(NG):
                    ins = pe.transpose(ps[:, g * P:(g + 1) * P],
                                       hot_flat[:, bass.ds((s.c * NG + g) * TAB, TURN)],
                                       ident16[:])
                ins.then_inc(sem("n_hot_ps"), 1)

            def node_body(s):
                if live(s, 1, NB):
                    p = s.back(1)
                    after(pe, "n_hot", p.c + 1)
                    after(pe, "n_nm", p.c - 1)
                    for h, res in enumerate(RES_BANKS[p.slot % 2]):
                        after(pe, "n_hc", 2 * p.c + h + 1)
                        pe.matmul(res[:], ident[:], flat(hc[:, p.slot % 2, h * G:(h + 1) * G]),
                                  start=True, stop=False, skip_group_check=True)
                        by_type(res, hot_t[:, p.slot, h], TAB_A, False, True).then_inc(sem("n_res"), 1)
                if live(s, 2, NB):
                    p = s.back(2)
                    for h in range(2):
                        after(pe, "n_y", 2 * p.c - 1 + h)
                        if h:
                            after(pe, "n_hot", min(p.c + 3, NB) if isinstance(p.c, int) else p.c + 3)
                        by_type(psum[2 + h], hot_t[:, p.slot, h], TAB_G, True, True).then_inc(sem("n_g"), 1)
                    for h in range(2):
                        after(pe, "n_out", 2 * p.c - 1 + h)
                        pe.matmul(psum[6 + h][:], ident[:], xa[:, p.slot, h * G:(h + 1) * G, XC],
                                  start=True, stop=False, skip_group_check=True)
                        by_type(psum[6 + h], hot_t[:, p.slot, h], TAB_B, False, True).then_inc(sem("n_xb"), 1)
                if live(s, -1, NB):
                    if live(s, 2, NB):
                        after(pe, "n_y", 2 * p.c + 2)
                    turn_hot(s.back(-1))

            turn_hot(Step(0, RING))
            pe.wait_ge(sem("rows_ready"), 1)
            for k in range(3):
                pe.transpose(psum[k][:, 0:LO], rows_f[0:LO, 0, k, :], ident[0:LO, 0:LO])
                pe.transpose(psum[k][:, LO:NT], rows_f[0:HI, 1, k, :], ident[0:HI, 0:HI])\
                    .then_inc(sem("cols_ps"), 1)
            pe.wait_ge(sem("index_ready"), 3)
            node_steps(pe, node_body)
            pe.wait_ge(sem("n_out"), 2 * NB)
            pe.wait_ge(sem("weights_ready"), 1)

            def project(ps, weights, tab_row, rows_m, hot, s):
                for t in range(T):
                    pe.matmul(ps[:], weights[:, t], rows_m[:, t], start=(t == 0), stop=False)
                return pe.matmul(ps[:], tab16[:, tab_row, :], hot, start=False, stop=True)

            def edge_body(s):
                c, b, a, z = s, s.back(1), s.back(2), s.back(3)
                if live(s, 1, NC):
                    after(pe, "e_hsm", b.c + 1)
                    after(pe, "e_prod", b.c)
                    project(psum[3], wk, TAB_K, hsm, hot_t[:, b.slot, 0], b).then_inc(sem("e_k"), 1)
                if live(s, 3, NC):
                    after(pe, "e_y", z.c)
                    by_type(psum[7], hot_t[:, z.slot, 1], TAB_G, True, True).then_inc(sem("e_g"), 1)
                if live(s, 1, NC):
                    after(pe, "e_hdm", b.c + 1)
                    after(pe, "e_te1", b.c)
                    project(psum[5], wq, TAB_Q, hdm, hot_t[:, b.slot, 1], b).then_inc(sem("e_q"), 1)
                if live(s, 0, NC):
                    after(pe, "e_h", c.c + 1)
                    after(pe, "e_hsm", c.c)
                    after(pe, "e_hdm", c.c)
                    for g in range(G):
                        pe.transpose(psum[0][:, g * P:(g + 1) * P], hs[:, g], ident[:])
                        pe.transpose(psum[1][:, g * P:(g + 1) * P], hd[:, g], ident[:])
                    after(pe, "e_tyb", 2 * c.c)
                    for k, row in enumerate((xs16[:, c.slot % 2], xd16[:, c.slot])):
                        for g in range(G):
                            ins = pe.transpose(psum[2][0:TURN, :].bitcast(BF16)[:, k * W + g * P:k * W + (g + 1) * P],
                                               row[:, g, 0:TURN], ident16[:])
                    ins.then_inc(sem("e_turned"), 1)
                if live(s, 3, NC):
                    after(pe, "e_sum", z.c + 1)
                    by_type(psum[6], hot_t[:, z.slot, 1], TAB_B, True, True).then_inc(sem("e_b"), 1)
                if live(s, 1, NC):
                    after(pe, "e_pm", b.c)
                    project(psum[4], wv, TAB_V, hsm, hot_t[:, b.slot, 0], b).then_inc(sem("e_v"), 1)
                if live(s, 0, NC):
                    after(pe, "e_hot", c.c + 1)
                    pe.matmul(psum[2][:], spread_type[:], hot_t[:, c.slot, 0], start=True, stop=True)\
                        .then_inc(sem("e_spread"), 1)
                    after(pe, "e_qs", c.c)
                    pe.matmul(psum[5][:], spread_type[:], hot_t[:, c.slot, 1], start=True, stop=True)\
                        .then_inc(sem("e_spread"), 1)
                if live(s, 1, NC):
                    after(pe, "e_km", b.c + 1)
                    for r in range(R):
                        ins = pe.matmul(psum[3][:], att_w[:, r], km[:, r], start=(r == 0), stop=(r == R - 1))
                    ins.then_inc(sem("e_rot"), 1)
                    after(pe, "e_vm", b.c + 1)
                    for r in range(R):
                        ins = pe.matmul(psum[4][:], msg_w[:, r], vm[:, r], start=(r == 0), stop=(r == R - 1))
                    ins.then_inc(sem("e_msg"), 1)
                    after(pe, "e_prod", b.c + 1)
                    after(pe, "e_tyb", 2 * (min(b.c + 2, NC) if isinstance(b.c, int) else b.c + 2))
                    pe.matmul(psum[5][:], head_ones[:], prod, start=True, stop=True).then_inc(sem("e_att"), 1)
                if live(s, 2, NC):
                    after(pe, "e_y2", a.c)
                    after(pe, "e_gm", a.c + 1)
                    for g in range(G):
                        cols = slice(g * P, (g + 1) * P)
                        for t in range(T):
                            pe.matmul(psum[6][:, cols], gm[:, t, cols], wa[:, t], start=(t == 0), stop=False)
                        ins = pe.matmul(psum[6][:, cols], hot_t[:, a.slot, 1, cols], tab16[:, TAB_A, :],
                                        start=False, stop=True)
                    ins.then_inc(sem("e_res"), 1)
            edge_steps(pe, edge_body)

        @block.vector
        def _(dve):
            chain = [0]

            def link(ins):
                chain[0] += 1
                ins.then_inc(sem("dve_prep"), 1)
                dve.wait_ge(sem("dve_prep"), chain[0])

            dve.memset(top[:, W:W + 1], 0.0)
            dve.memset(run[:, :, W - 1:W], 0.0)
            dve.memset(hot_flat[:, NB * NG * TAB:], 0.0)
            dve.memset(dstb[:, 0, 0:1], -1).then_inc(sem("dve_init"), 1)

            def one_hot(hot, types, n):
                v = hot.rearrange("p n (k t) -> p n k t", k=PARTS)
                for t in range(T):
                    ins = dve.tensor_scalar(v[:, :, :, t], types.unsqueeze(2).to_broadcast([P, n, PARTS]),
                                            float(t), None, ALU.is_equal)
                return ins

            dve.wait_ge(sem("types_in"), 32)
            one_hot(hot_n, nt_all[:], NB * NG).then_inc(sem("hot_n_ready"), 1)
            dve.wait_ge(sem("gate_exp"), 2)
            link(dve.tensor_scalar(gate[:, 1, :], gate[:, 1, :], 1.0, None, ALU.add))
            link(dve.reciprocal(gate[:, 2, :], gate[:, 1, :]))
            link(dve.tensor_scalar(gate[:, 3, :], gate[:, 2, :], -1.0, 1.0, ALU.mult, ALU.add))
            link(dve.tensor_scalar(gate_row[:, 1:2], gate_row[:, 1:2], 1.0, None, ALU.add))
            link(dve.reciprocal(gate_row[:, 2:3], gate_row[:, 1:2]))
            dve.wait_ge(sem("hot_n_ready"), 1)
            link(dve.tensor_scalar(keep_n[:], hot_n[:, :, 0], gate[:, 3, 0:1], None, ALU.mult))
            link(dve.scalar_tensor_tensor(keep_n[:], hot_n[:, :, 1], gate[:, 3, 1:2], keep_n[:], ALU.mult, ALU.add))
            dve.scalar_tensor_tensor(keep_n[:], hot_n[:, :, 2], gate[:, 3, 2:3], keep_n[:], ALU.mult, ALU.add)\
                .then_inc(sem("keep_ready"), 1)
            dve.wait_ge(sem("const"), 7)

            def prepare_tables():
                dve.wait_ge(sem("tab_in"), 16 * PARTS * NTAB)
                link(dve.tensor_scalar(tab[:, TAB_A, :], tab[:, TAB_A, :], gate_row[:, 2:3], None, ALU.mult))
                link(dve.tensor_copy(tab_hi, tab[:]))
                link(dve.tensor_tensor(tab_r1, tab[:], tab_hi, ALU.subtract))
                link(dve.tensor_copy(tab_mid, tab_r1))
                link(dve.tensor_tensor(tab_r2, tab_r1, tab_mid, ALU.subtract))
                link(dve.tensor_copy(tab_lo, tab_r2))
                link(dve.tensor_scalar(tab16[:], tab_hi, part_mask[:, 0:1], None, ALU.mult))
                for part, t in ((1, tab_mid), (2, tab_lo)):
                    link(dve.scalar_tensor_tensor(tab16[:], t, part_mask[:, part:part + 1], tab16[:],
                                                  ALU.mult, ALU.add))
                dve.scalar_tensor_tensor(spread_type[:], type_of_row[:], float(T - 1), type_of_row[:],
                                         ALU.is_le, ALU.mult).then_inc(sem("tables_ready"), 1)

            def prepare_edges():
                dve.wait_ge(sem("index_in"), 16 * 9)
                dve.tensor_copy(rows_f, rows_i[:]).then_inc(sem("rows_ready"), 1)
                dve.wait_ge(sem("cols_ps"), 3)
                for k in range(3):
                    last = dve.tensor_copy(cols_f[:, k, :], psum[k][:, 0:NT])
                link(last)
                for k in range(2):
                    dve.tensor_scalar(index[:, :, k, :], cols_f[:, k, :].rearrange("p (c g) -> p c g", g=G),
                                      0.0, None, ALU.max).then_inc(sem("index_ready"), 1)
                link(dve.tensor_tensor(last_of_run[:], cols_f[:, 1, :], cols_f[:, 2, :], ALU.is_equal))
                dve.scalar_tensor_tensor(index[:, :, 2, :], last_of_run[:].rearrange("p (c g) -> p c g", g=G),
                                         float(SKIP_ROW), cols_f[:, 1, :].rearrange("p (c g) -> p c g", g=G),
                                         ALU.mult, ALU.add).then_inc(sem("index_ready"), 1)
                dve.wait_ge(sem("weights_in"), W_LOADS)
                link(dve.tensor_scalar(pri[:], pri[:], 1.0 / math.sqrt(DK), None, ALU.mult))
                per_head = lambda t: t.rearrange("p (h f) -> p h f", h=H)
                for r in range(R):
                    for to, from_, scale in ((att_w, att_c, pri[:, r:r + 1]), (msg_w, msg_c, 1.0)):
                        dve.scalar_tensor_tensor(per_head(to[:, r]),
                                                 from_[:, r].unsqueeze(1).to_broadcast([P, H, DK]), scale,
                                                 per_head(head_ones[:]), ALU.mult, ALU.mult)
                for t in range(T):
                    ins = dve.tensor_scalar(wa[:, t], wa[:, t], gate[:, 2, t:t + 1], None, ALU.mult)
                ins.then_inc(sem("weights_ready"), 1)

            def stats(rows_of, n, b, mv, name, count, ready=None):
                for g in range(n):
                    if ready:
                        ready(g)
                    ins = dve.bn_stats(b[:, g], rows_of(g))
                ins.then_inc(sem(name + "_parts"), 1)
                after(dve, name + "_parts", count + 1)
                hold(dve, "dve_turns")
                for g in range(n):
                    ins = dve.bn_aggr(mv[:, g], b[:, g])
                ins.then_inc(sem(name), 1)

            def node_body(s):
                if live(s, 0, NB):
                    after(dve, f"x_in{s.slot}", 16 * (s.round + 1))
                    after(dve, "n_sc1", s.c)
                    dve.tensor_copy(xa16[:, s.slot, :, 0:TAB], hot_n[:, bass.ds(s.c * NG, NG), :]).then_inc(sem("n_type"), 1)
                    stats(lambda g: xa[:, s.slot, g, XC], NG, bst, mv1, "n_mv1", s.c)
                    if isinstance(s.c, int) and s.c == 0:
                        prepare_tables()
                        prepare_edges()
                if live(s, 1, NB):
                    p = s.back(1)
                    after(dve, "n_sc2", p.c)
                    res = RES_BANKS[p.slot % 2]
                    stats(lambda g: res[g // G][:, g % G * P:(g % G + 1) * P], NG, bst2, mv2, "n_mv2", p.c,
                          lambda g: after(dve, "n_res", 2 * p.c + g // G + 1) if g % G == 0 else None)
                if live(s, 2, NB):
                    p = s.back(2)
                    after(dve, "n_nm", p.c + 1)
                    halves = [flat(nm[:, h * G:(h + 1) * G]) for h in range(2)]
                    for h in range(2):
                        after(dve, "n_g", 2 * p.c + h + 1)
                        dve.tensor_tensor(halves[h], halves[h], psum[2 + h][:], ALU.mult).then_inc(sem("n_y"), 1)
                    after(dve, f"o_out{p.slot % 2}", 16 * (2 * p.round + p.slot // 2))
                    for h, bank in enumerate((6, 7)):
                        after(dve, "n_y", 2 * p.c + h + 1)
                        after(dve, "n_xb", 2 * p.c + h + 1)
                        dve.tensor_tensor(flat(oa[:, p.slot % 2, h * G:(h + 1) * G]), halves[h], psum[bank][:],
                                          ALU.add).then_inc(sem("n_out"), 1)
            node_steps(dve, node_body)

            def mask(out_ap, types, value, rows_in):
                return dve.scalar_tensor_tensor(out_ap, types, float(value), rows_in, ALU.is_equal, ALU.mult)

            def edge_body(s):
                c, b, a, z = s, s.back(1), s.back(2), s.back(3)
                if live(s, 1, NC):
                    after(dve, "e_turned", b.c + 1)
                    after(dve, "e_tyb", 2 * (b.c + 1))
                    after(dve, "e_q", b.c)
                    for t in range(T):
                        ins = mask(hdm[:, t], tyb_d[:, b.slot], t, psum[1][:])
                    ins.then_inc(sem("e_hdm"), 1)
                if live(s, 2, NC):
                    dve.tensor_copy(top[:, 0:1], top[:, W:W + 1])
                    after(dve, "e_cut", a.c + 1)
                    after(dve, "e_att", a.c + 1)
                    at = a.slot % 2
                    dve.tensor_tensor_scan(top[:, 1:W + 1], cut[:, at], psum[5][:], top[:, W:W + 1],
                                           ALU.add, ALU.max).then_inc(sem("e_top"), 1)
                    after(dve, "e_top", a.c + 1)
                    dve.tensor_tensor(te[:, 1], psum[5][:], top[:, 1:W + 1], ALU.subtract).then_inc(sem("e_te1"), 1)
                if live(s, 3, NC):
                    after(dve, "e_res", z.c + 1)
                    after(dve, "e_hc", z.c + 1)
                    dve.tensor_tensor(hd_keep, hd_keep, psum[6][:], ALU.add).then_inc(sem("e_sum"), 1)
                if live(s, 2, NC):
                    after(dve, "e_left", a.c + 1)
                    dve.tensor_tensor(te[:, 0], from_left, top[:, 1:W + 1], ALU.subtract).then_inc(sem("e_te"), 1)
                if live(s, 3, NC):
                    after(dve, "e_sum", z.c + 1)
                    stats(lambda g: hd_keep[:, g * P:(g + 1) * P], G, bst2, mv2, "e_mv2", z.c)
                if live(s, 1, NC):
                    after(dve, f"e_in{b.slot}", 32 * (b.round + 1))
                    after(dve, "e_k", b.c + 1)
                    for r in range(R):
                        ins = mask(km[:, r], etb[:, b.slot % 2], r, psum[3][:])
                    ins.then_inc(sem("e_km"), 1)
                if live(s, 2, NC):
                    after(dve, "e_ce", a.c + 1)
                    after(dve, "e_msg", a.c + 1)
                    dve.tensor_tensor(pm, psum[4][:], ce[:, 1], ALU.mult).then_inc(sem("e_pm"), 1)
                    dve.tensor_tensor_scan(run[:, 1], ce[:, 0], ce[:, 1], run[:, 1, W - 1:W],
                                           ALU.mult, ALU.add).then_inc(sem("e_wsum"), 1)
                    after(dve, "e_pm", a.c + 1)
                    dve.tensor_tensor_scan(run[:, 0], ce[:, 0], pm, run[:, 0, W - 1:W],
                                           ALU.mult, ALU.add).then_inc(sem("e_run"), 1)
                if live(s, 3, NC):
                    after(dve, "e_nm", z.c + 1)
                    after(dve, "e_g", z.c + 1)
                    dve.tensor_tensor(yge, nme, psum[7][:], ALU.mult).then_inc(sem("e_y"), 1)
                    after(dve, "e_y", z.c + 1)
                    after(dve, "e_b", z.c + 1)
                    after(dve, "e_out", z.c - 1)
                    dve.tensor_tensor(yge2[:, z.slot % 2], yge, psum[6][:], ALU.add).then_inc(sem("e_y2"), 1)
                if live(s, 2, NC):
                    after(dve, "e_inv0", a.c + 1)
                    after(dve, "e_wsum", a.c + 1)
                    dve.scalar_tensor_tensor(nt1, run[:, 1], DEN_EPS, inv0, ALU.add, ALU.mult)\
                        .then_inc(sem("e_nt"), 1)
                    after(dve, "e_nt", 2 * a.c + 1)
                    dve.scalar_tensor_tensor(nt2, nt1, 2.0, inv0, ALU.subtract, ALU.mult).then_inc(sem("e_nt"), 1)
                    after(dve, "e_nt", 2 * a.c + 2)
                    after(dve, "e_run", a.c + 1)
                    dve.scalar_tensor_tensor(ag, nt2, -1.0, run[:, 0], ALU.mult, ALU.mult)\
                        .then_inc(sem("e_ag"), 1)
                if live(s, 1, NC):
                    after(dve, "e_v", b.c + 1)
                    for r in range(R):
                        ins = mask(vm[:, r], etb[:, b.slot % 2], r, psum[4][:])
                    ins.then_inc(sem("e_vm"), 1)
                    after(dve, "e_rot", b.c + 1)
                    after(dve, "e_qs", b.c + 1)
                    dve.tensor_tensor(prod, psum[3][:], qs, ALU.mult).then_inc(sem("e_prod"), 1)
                if live(s, 2, NC):
                    after(dve, "e_ge", a.c + 1)
                    for t in range(T):
                        ins = mask(gm[:, t], tyb_d[:, a.slot], t, ge)
                    ins.then_inc(sem("e_gm"), 1)
                if live(s, 0, NC):
                    after(dve, "e_turned", c.c + 1)
                    after(dve, "e_tyb", 2 * c.c + 1)
                    after(dve, "e_v", c.c)
                    for t in range(T):
                        ins = mask(hsm[:, t], tyb_s[:], t, psum[0][:])
                    ins.then_inc(sem("e_hsm"), 1)
            edge_steps(dve, edge_body)


TABLE_ROW = 144

_INS = ["x", "src", "dst", "edge_type_4", "node_type_3"] + [
    "L0_gnn_" + n for n in ("Wk", "bk", "Wq", "bq", "Wv", "bv", "Wa", "ba", "rel_pri", "rel_att",
                            "rel_msg", "skip", "ln_g", "ln_b")]


def kernel(**inputs):
    import numpy as np
    import concourse.bacc as bacc
    from concourse.bass_utils import run_bass_kernel_spmd

    nc = bacc.Bacc("TRN2", target_bir_lowering=False, num_devices=1)
    arrays, args = {}, []
    for name in _INS:
        a = np.ascontiguousarray(inputs[name])
        arrays["in_" + name] = a
        args.append(nc.dram_tensor("in_" + name, a.shape, mybir.dt.from_np(a.dtype), kind="ExternalInput").ap())
    shape = inputs["x"].shape
    args.append(nc.dram_tensor("out_x", shape, F32, kind="ExternalOutput").ap())
    table = nc.dram_tensor("node_table", (shape[0], TABLE_ROW), F32, kind="Internal").ap()
    gnn_layer(nc, *args[:-1], table, args[-1])
    r = run_bass_kernel_spmd(nc, [arrays], core_ids=[0])
    return r.results[0]["out_x"]
```
